# Optimizing a Trainium2 kernel written in Bass

```python
import numpy as np
import jax
import jax.numpy as jnp

def _softmax(x, axis=-1):
    return jax.nn.softmax(x, axis=axis)

def _gelu(x):
    return jax.nn.gelu(x, approximate=True)

def _silu(x):
    return jax.nn.silu(x)

def _sigmoid(x):
    return jax.nn.sigmoid(x)

def _layernorm(x, axis=-1, eps=1e-05):
    m = jnp.mean(x, axis=axis, keepdims=True)
    v = jnp.var(x, axis=axis, keepdims=True)
    return (x - m) / jnp.sqrt(v + eps)

def _scatter_add(tgt, idx, src, axis=0):
    return tgt.at[idx].add(src)

def _segment_sum(src, seg, n):
    return jax.ops.segment_sum(src, seg, n)
kernel_name = 'mk_prb_d1_jaxref_r4_4ef713'

def setup_inputs(seed: int=0):
    np.random.seed(seed)
    _w = jnp.asarray

    def _L0_attn_setup():
        import jax, jax.numpy as jnp
        import numpy as np
        H = 1024
        D = H // 4
        key = jax.random.key(seed)
        k1, k2, k3, k4, k5 = jax.random.split(key, 5)
        x = jax.random.normal(k1, (4, 1024, H), dtype=jnp.float32)
        s_in = 1.0 / np.sqrt(H)
        Wqkv = jax.random.normal(k2, (H, 3 * D), dtype=jnp.float32) * s_in
        bqkv = jax.random.normal(k3, (3 * D,), dtype=jnp.float32) * 0.01
        Wo = jax.random.normal(k4, (D, H), dtype=jnp.float32) * (1.0 / np.sqrt(D))
        bo = jax.random.normal(k5, (H,), dtype=jnp.float32) * 0.01
        return {'x': x, 'Wqkv': Wqkv, 'bqkv': bqkv, 'Wo': Wo, 'bo': bo}
    _L0_attn_in = _L0_attn_setup()

    def _L0_ffn_setup():
        import jax, jax.numpy as jnp
        import numpy as np
        HIDDEN = 1024
        INTER = 2752

        def _ternary_quantize(w):
            scale = jnp.mean(jnp.abs(w))
            return jnp.clip(jnp.round(w / scale), -1.0, 1.0) * scale
        key = jax.random.key(seed)
        kx, kg, ku, kd = jax.random.split(key, 4)
        x = jax.random.normal(kx, (2, 512, HIDDEN), dtype=jnp.float32)
        w_gate = _ternary_quantize(jax.random.normal(kg, (INTER, HIDDEN), dtype=jnp.float32) * 0.02)
        w_up = _ternary_quantize(jax.random.normal(ku, (INTER, HIDDEN), dtype=jnp.float32) * 0.02)
        w_down = _ternary_quantize(jax.random.normal(kd, (HIDDEN, INTER), dtype=jnp.float32) * 0.02)
        return {'x': x, 'w_gate': w_gate, 'w_up': w_up, 'w_down': w_down}
    _L0_ffn_in = _L0_ffn_setup()
    _d = {'L0_attn_x': _L0_attn_in['x'], 'L0_attn_Wqkv': _L0_attn_in['Wqkv'], 'L0_attn_bqkv': _L0_attn_in['bqkv'], 'L0_attn_Wo': _L0_attn_in['Wo'], 'L0_attn_bo': _L0_attn_in['bo'], 'L0_ffn_w_gate': _L0_ffn_in['w_gate'], 'L0_ffn_w_up': _L0_ffn_in['w_up'], 'L0_ffn_w_down': _L0_ffn_in['w_down']}
    _x0 = _d['L0_attn_x']
    _d['L0_attn_x'] = jax.random.normal(jax.random.fold_in(jax.random.key(seed), 1), (4, 512, 1024), dtype=_x0.dtype)
    del _x0
    return _d

def reference(L0_attn_x, L0_attn_Wqkv, L0_attn_bqkv, L0_attn_Wo, L0_attn_bo, L0_ffn_w_gate, L0_ffn_w_up, L0_ffn_w_down):

    def _L0_attn_ref(x, Wqkv, bqkv, Wo, bo):
        import jax, jax.numpy as jnp
        import numpy as np
        H = 1024
        D = H // 4
        B, S, C = x.shape
        d = C // 4
        qkv = jnp.einsum('bsc,cf->bsf', x, Wqkv) + bqkv
        qkv = qkv.reshape(B, S, 3, d)
        q, k, v = (qkv[:, :, 0], qkv[:, :, 1], qkv[:, :, 2])
        scale = 1.0 / jnp.sqrt(jnp.float32(d)).astype(x.dtype)
        attn = jnp.einsum('bqd,bkd->bqk', q, k) * scale
        attn = jax.nn.softmax(attn, axis=-1)
        out = jnp.einsum('bqk,bkd->bqd', attn, v)
        return jnp.einsum('bqd,dc->bqc', out, Wo) + bo

    def _L0_ffn_ref(x, w_gate, w_up, w_down):
        import jax, jax.numpy as jnp
        import numpy as np
        HIDDEN = 1024
        INTER = 2752

        def _ternary_quantize(w):
            scale = jnp.mean(jnp.abs(w))
            return jnp.clip(jnp.round(w / scale), -1.0, 1.0) * scale
        xf = x.astype(jnp.float32) / 128.0
        gate = jnp.einsum('bsh,ih->bsi', xf, w_gate)
        up = jnp.einsum('bsh,ih->bsi', xf, w_up)
        inter = jax.nn.silu(gate) * up
        inter_q = jnp.trunc(jnp.clip(inter * 128.0, -128.0, 127.0)).astype(jnp.int8)
        down = jnp.einsum('bsi,hi->bsh', inter_q.astype(jnp.float32), w_down)
        out = jnp.trunc(jnp.clip(down * 128.0, -128.0, 127.0)).astype(jnp.int8)
        return out
    x = L0_attn_x
    xn = _layernorm(x, axis=-1)
    x = x + _L0_attn_ref(xn, L0_attn_Wqkv, L0_attn_bqkv, L0_attn_Wo, L0_attn_bo) + _L0_ffn_ref(xn, L0_ffn_w_gate, L0_ffn_w_up, L0_ffn_w_down)
    return x

_drawn_inputs = setup_inputs


def setup_inputs(seed=0):
    import zlib

    import numpy as np

    out = dict(_drawn_inputs(seed))
    spreads = {}
    factors = {'L0_attn_bqkv': 5.074, 'L0_attn_bo': 5.771}
    for name, (base, spread) in spreads.items():
        noise = np.random.default_rng([zlib.crc32(name.encode()), seed]).standard_normal(out[name].shape)
        drawn = base * np.exp(spread * noise) if base else spread * noise
        out[name] = jnp.asarray(drawn.astype(out[name].dtype))
    for name, factor in factors.items():
        out[name] = (out[name] * factor).astype(out[name].dtype)
    return out
```

```python
from contextlib import ExitStack

import concourse.bass as bass
from concourse import mybir

ALU = mybir.AluOpType
ACT = mybir.ActivationFunctionType
F32 = mybir.dt.float32
F16 = mybir.dt.float16
I32 = mybir.dt.int32
AX_X = mybir.AxisListType.X
ABSMAX = bass.bass_isa.ReduceOp.absmax

P = 128
W_UNIT = 8192.0
X_UNIT = 1024.0
HALVES = 2.0 ** 22
HALVES_UP = HALVES - 0.25
HALVES_DOWN = HALVES - 0.75
ONES = 2.0 ** 23
ONES_DOWN = 2.0 ** 23 + 1
TINY = 1e-30
EPS = 1e-5
ACT_Q = 128.0


def build(nc, x_tok, x_feat, w_qkv, b_qk, b_v, w_gu, w_gu_last, w_down, w_o, b_o, out):
    TOK, H = x_tok.shape
    KT = H // P
    CH = 512
    B = TOK // CH
    TT = CH // P
    NF = w_qkv.shape[1]
    DT = NF // 3
    D = DT * P
    NI = w_gu.shape[0]
    HALF = P // 2
    IT = NI + 1
    HT = H // P
    SOFT = float(D) ** -0.5
    GU = KT * P
    DN = IT * P

    with ExitStack() as ctx:
        def sb(name, shape, dt):
            return ctx.enter_context(nc.sbuf_tensor(name, shape, dt))

        def sem(name):
            return ctx.enter_context(nc.semaphore(name))

        xn = sb("xn", [P, B, 2, KT, CH], F16)
        act_q = sb("act_q", [P, IT, TOK], F16)
        attn_t = sb("attn_t", [P, DT, TOK], F32)
        gu_in = sb("gu_in", [P, 2, GU], F32)
        gu_hi = sb("gu_hi", [P, 2, 2, KT, P], F16)
        gu_lo = sb("gu_lo", [P, 2, 2, KT, P], F16)
        sig = sb("sig", [P, 2, CH], F32)
        mag = sb("mag", [P, 2, CH], F32)
        sgn = sb("sgn", [P, 2, CH], F16)
        rnd = sb("rnd", [P, CH], F32)
        tmp = sb("tmp", [P, CH], F32)
        ident = sb("ident", [P, P], F32)
        eps = sb("eps", [P, 1], F32)
        bqk = sb("bqk", [P, 2 * DT], F32)
        bo = sb("bo", [P, HT], F32)
        wmax = sb("wmax", [P, 2], F32)
        gmax = sb("gmax", [P, 2], F32)
        wtop = sb("wtop", [P, 2], F32)
        winv = sb("winv", [P, 2], F32)
        to_unit = sb("to_unit", [P, 2, 2], F32)
        to_unit_n = sb("to_unit_n", [P, 2, 2], F32)
        unit = sb("unit", [P, 2, 2], F32)
        descale = sb("descale", [P, 2, 2], F32)
        lo_sum = sb("lo_sum", [P, 2, 2], F32)
        lo_top = sb("lo_top", [P, 2], F32)
        has_lo = sb("has_lo", [P, 2], F32)
        stats = sb("stats", [P, TT, 2, 6], F32)
        mean_var = sb("mean_var", [P, TT, 2], F32)
        std = sb("std", [P, TT], F32)
        rstd = sb("rstd", [P, TT], F32)
        rstd_x = sb("rstd_x", [P, TT], F32)
        neg_max = sb("neg_max", [P, TT], F32)
        soft_bias = sb("soft_bias", [P, TT], F32)
        row_sum = sb("row_sum", [P, TT], F32)
        row_inv = sb("row_inv", [P, TT], F32)
        fence = sb("fence", [P, 1], F32)
        bo_now = sb("bo_now", [P, 2], F32)

        a32 = act_q[:, :, :].rearrange("p a b -> p (a b)").bitcast(F32)
        place = [0]

        def in_a(n):
            place[0] += n
            assert place[0] <= IT * TOK // 2
            return a32[:, place[0] - n:place[0]]

        wqkv_in = in_a(NF * GU)
        wqkv_hi = in_a(NF * GU // 2).bitcast(F16).rearrange("p (f k c) -> p f k c", f=NF, k=KT)
        wqkv_lo = in_a(NF * GU // 2).bitcast(F16).rearrange("p (f k c) -> p f k c", f=NF, k=KT)
        x_in = in_a(TT * H).rearrange("p (t h) -> p t h", t=TT)
        q_t = in_a(DT * CH).rearrange("p (d s) -> p d s", d=DT)
        k_t = in_a(DT * CH).rearrange("p (d s) -> p d s", d=DT)
        v = in_a(TT * D).rearrange("p (t d) -> p t d", t=TT)
        bv = in_a(D)
        prob = wqkv_in[:, 0:TT * CH].rearrange("p (t s) -> p t s", t=TT)
        prob_t = wqkv_in[:, TT * CH:2 * TT * CH].rearrange("p (t s) -> p t s", t=TT)

        def in_xn(b):
            return xn[:, b, :, :, :].rearrange("p a k s -> p (a k s)")

        dn_in = in_xn(0).bitcast(F32)[:, 0:DN]
        wo_in = in_xn(0).bitcast(F32)[:, DN:DN + 2 * DT * P].rearrange("p (b d c) -> p b d c", b=2, d=DT)
        dn_hi = [in_xn(1 + i)[:, 0:DN].rearrange("p (i c) -> p i c", i=IT) for i in range(2)]
        dn_lo = [in_xn(1 + i)[:, DN:2 * DN].rearrange("p (i c) -> p i c", i=IT) for i in range(2)]
        xf_in = [in_xn(3).bitcast(F32)[:, i * TOK:(i + 1) * TOK] for i in range(2)]
        out_sb = [gu_hi[:, :, :, :, :].rearrange("p a b k c -> p (a b k c)").bitcast(F32)[:, 0:TOK],
                  gu_lo[:, :, :, :, :].rearrange("p a b k c -> p (a b k c)").bitcast(F32)[:, 0:TOK]]

        ps = ctx.enter_context(nc.psum_tensor("ps", [P, 8, CH], F32))

        ident0, ident_ok, eps_ok = sem("ident0"), sem("ident_ok"), sem("eps_ok")
        wqkv_in_ok, small_in = sem("wqkv_in_ok"), sem("small_in")
        x_in_ok = [sem(f"x_in_ok{i}") for i in range(2)]
        gu_in_ok, dn_in_ok = sem("gu_in_ok"), sem("dn_in_ok")
        wo_in_ok = [sem(f"wo_in_ok{i}") for i in range(2)]
        xf_in_ok = [sem(f"xf_in_ok{i}") for i in range(2)]
        stored = [sem(f"stored{i}") for i in range(2)]
        wmax_ok, gmax_ok, wtop_ok, winv_ok, scales_ok = (
            sem("wmax_ok"), sem("gmax_ok"), sem("wtop_ok"), sem("winv_ok"), sem("scales_ok"))
        whi_ok, werr_ok, wlo_ok = sem("whi_ok"), sem("werr_ok"), sem("wlo_ok")
        lo_sum_ok, lo_top_ok, has_lo_ok = sem("lo_sum_ok"), sem("lo_top_ok"), sem("has_lo_ok")
        stats_ok, mv_ok, std_ok, rstd_ok, rstd_x_ok, norm_ok = (
            sem("stats_ok"), sem("mv_ok"), sem("std_ok"), sem("rstd_ok"), sem("rstd_x_ok"), sem("norm_ok"))
        xt_ready, xhi_ok, xlo_ok = sem("xt_ready"), sem("xhi_ok"), sem("xlo_ok")
        qk_ready, qk_ok, v_ready, v_ok = sem("qk_ready"), sem("qk_ok"), sem("v_ready"), sem("v_ok")
        s_ready, max_ok, bias_ok, exp_ok = sem("s_ready"), sem("max_ok"), sem("bias_ok"), sem("exp_ok")
        inv_ok, prob_ok, pt_ready, pt_ok = sem("inv_ok"), sem("prob_ok"), sem("pt_ready"), sem("pt_ok")
        pv_ready, attn_ok = sem("pv_ready"), sem("attn_ok")
        gu_ready, silu_ok, inter_ok, mag_ok, sgn_ok = (
            sem("gu_ready"), sem("silu_ok"), sem("inter_ok"), sem("mag_ok"), sem("sgn_ok"))
        rnd_ok, floor_ok, signed_ok, q_ok = sem("rnd_ok"), sem("floor_ok"), sem("signed_ok"), sem("q_ok")
        dn_ready, res_ok, out_ok, bo_ok = sem("dn_ready"), sem("res_ok"), sem("out_ok"), sem("bo_ok")

        JOBS_B = IT * B
        QKV_B = 1
        DN_B = 1 + IT

        def parts(blk):
            return 2 * blk + (NF - 2)

        block = ctx.enter_context(nc.Block())

        @block.sync
        def _(sp):
            def load_x(b):
                for half in range(2):
                    sp.dma_start(x_in[:, 2 * half:2 * half + 2, :],
                                 x_tok[bass.ds(b * CH + half * 2 * P, 2 * P), :].rearrange("(t p) h -> p t h", p=P)
                                 ).then_inc(x_in_ok[half], 16)

            load_x(0)
            sp.dma_start(wqkv_in, w_qkv.rearrange("p f n -> p (f n)")).then_inc(wqkv_in_ok, 16)
            sp.dma_start(bqk[:, :], b_qk).then_inc(small_in, 16)
            sp.dma_start(bo[:, :], b_o).then_inc(small_in, 16)
            sp.dma_start(bv, b_v.partition_broadcast(P)).then_inc(small_in, 16)
            sp.dma_start(gu_in[:, :, :], w_gu[0]).then_inc(gu_in_ok, 16)
            with sp.Fori(1, B) as b:
                sp.wait_ge(xt_ready, b * TT)
                load_x(b)
            with sp.Fori(1, NI) as t:
                sp.wait_ge(lo_sum_ok, 2 * t)
                sp.dma_start(gu_in[:, :, :], w_gu[bass.ds(t, 1)].rearrange("a p g n -> p (a g) n")).then_inc(gu_in_ok, 16)
            sp.wait_ge(lo_sum_ok, 2 * NI)
            sp.dma_start(gu_in[:, 0, :], w_gu_last).then_inc(gu_in_ok, 16)
            sp.wait_ge(gu_ready, NI * B + 1)
            sp.dma_start(dn_in, w_down[0]).then_inc(dn_in_ok, 16)
            sp.dma_start(wo_in[:, 0, :, :], w_o[0]).then_inc(wo_in_ok[0], 16)
            sp.wait_ge(gu_ready, NI * B + B)
            sp.dma_start(xf_in[0], x_feat[0]).then_inc(xf_in_ok[0], 16)

            def load_down(h, par):
                sp.wait_ge(lo_sum_ok, 2 * h + 2 * IT)
                sp.dma_start(dn_in, w_down[bass.ds(h, 1)].rearrange("a p n -> p (a n)")).then_inc(dn_in_ok, 16)
                sp.dma_start(wo_in[:, par, :, :],
                             w_o[bass.ds(h, 1)].rearrange("a p d c -> p (a d) c")).then_inc(wo_in_ok[par], 16)
                sp.dma_start(xf_in[par], x_feat[bass.ds(h, 1)].rearrange("a p n -> p (a n)")).then_inc(xf_in_ok[par], 16)

            def store(h, par):
                for c in range(B):
                    sp.wait_ge(out_ok, B * h + (c + 1))
                    sp.dma_start(out[bass.ds(h, 1)].rearrange("a p n -> p (a n)")[:, c * CH:(c + 1) * CH],
                                 out_sb[par][:, c * CH:(c + 1) * CH]).then_inc(stored[par], 16)

            load_down(1, 1)
            store(0, 0)
            with sp.Fori(0, (HT - 1 - 1) // 2) as pair:
                h = pair * 2 + 1
                load_down(h + 1, 0)
                store(h, 1)
                load_down(h + 2, 1)
                store(h + 1, 0)
            store(HT - 1, 1)
            for par in range(2):
                sp.wait_ge(stored[par], 16 * B * HT // 2)

        @block.gpsimd
        def _(pool):
            nc.gpsimd.memset(ident[:, :], 0.0).then_inc(ident0, 1)
            nc.gpsimd.memset(eps[:, :], EPS).then_inc(eps_ok, 1)
            pool.wait_ge(ident0, 1)
            nc.gpsimd.affine_select(out=ident[:, :], in_=ident[:, :], compare_op=ALU.not_equal, fill=1.0,
                                    base=0, pattern=[[-1, P]], channel_multiplier=1).then_inc(ident_ok, 1)
            for n in range(1 + IT + HT):
                pool.wait_ge(wmax_ok, n + 1)
                nc.gpsimd.partition_all_reduce(gmax[:, :], wmax[:, :], P, ABSMAX).then_inc(gmax_ok, 1)
                if n >= QKV_B:
                    m, par = n - QKV_B, (n - QKV_B) % 2
                    pool.wait_ge(lo_sum_ok, 2 * m + 2)
                    nc.gpsimd.partition_all_reduce(lo_top[:, :], lo_sum[:, par, :], P, ABSMAX).then_inc(lo_top_ok, 1)
                    pool.wait_ge(lo_top_ok, m + 1)
                    nc.gpsimd.tensor_tensor(has_lo[:, par:par + 1], lo_top[:, 0:1], lo_top[:, 1:2],
                                            ALU.add).then_inc(has_lo_ok, 1)

        @block.tensor
        def _(pe):
            def xpart(b, part, k, lo, n):
                if isinstance(b, int):
                    return xn[:, b, part, k, lo:lo + n]
                return xn[:, bass.ds(b, 1), part, k, lo:lo + n].rearrange("p a s -> p (a s)")

            def transposes(b, after=True):
                for t in range(TT):
                    pe.wait_ge(norm_ok, b * TT + (t + 1))
                    if t >= 2:
                        pe.wait_ge(xhi_ok, b * TT + (t - 1))
                        pe.wait_ge(xlo_ok, b * TT + (t - 1))
                    for k in range(KT):
                        mm = nc.tensor.transpose(ps[:, 2 * (t % 2) + k // 4, (k % 4) * P:(k % 4 + 1) * P],
                                                 x_in[:, t, k * P:(k + 1) * P], ident[:, :])
                    mm.then_inc(xt_ready, 1)

            def queries_keys(b):
                pe.wait_ge(xhi_ok, b * TT + TT)
                pe.wait_ge(xlo_ok, b * TT + TT)
                for f in range(2 * DT):
                    for k in range(KT):
                        nc.tensor.matmul(ps[:, f, :], wqkv_hi[:, f, k, :], xpart(b, 0, k, 0, CH),
                                         start=(k == 0), stop=False)
                        nc.tensor.matmul(ps[:, f, :], wqkv_hi[:, f, k, :], xpart(b, 1, k, 0, CH),
                                         start=False, stop=False)
                        mm = nc.tensor.matmul(ps[:, f, :], wqkv_lo[:, f, k, :], xpart(b, 0, k, 0, CH),
                                              start=False, stop=(k == KT - 1))
                    mm.then_inc(qk_ready, 1)

            def values(b):
                for t in range(TT):
                    dst = ps[:, 2 + t // 2, (t % 2) * D:(t % 2 + 1) * D]
                    for k in range(KT):
                        nc.tensor.matmul(dst, xpart(b, 0, k, t * P, P), wqkv_hi[:, 2 * DT:NF, k, :],
                                         start=(k == 0), stop=False)
                        nc.tensor.matmul(dst, xpart(b, 0, k, t * P, P), wqkv_lo[:, 2 * DT:NF, k, :],
                                         start=False, stop=False)
                        mm = nc.tensor.matmul(dst, xpart(b, 1, k, t * P, P), wqkv_hi[:, 2 * DT:NF, k, :],
                                              start=False, stop=(k == KT - 1))
                    if t % 2:
                        mm.then_inc(v_ready, 1)

            def scores(b):
                pe.wait_ge(qk_ok, b * 4 + 4)
                for t in range(TT):
                    for d in range(DT):
                        mm = nc.tensor.matmul(ps[:, 4 + t, :], q_t[:, d, t * P:(t + 1) * P], k_t[:, d, :],
                                              start=(d == 0), stop=(d == DT - 1))
                    mm.then_inc(s_ready, 1)

            def attend(b):
                for t in range(TT):
                    pe.wait_ge(prob_ok, b * TT + (t + 1))
                    for j in range(TT):
                        mm = nc.tensor.transpose(ps[:, 4 + t, j * P:(j + 1) * P],
                                                 prob[:, t, j * P:(j + 1) * P], ident[:, :])
                    mm.then_inc(pt_ready, 1)
                pe.wait_ge(pt_ok, b * TT + TT)
                pe.wait_ge(v_ok, b * TT + TT)
                for d in range(DT):
                    for j in range(TT):
                        mm = nc.tensor.matmul(ps[:, d, :], v[:, j, d * P:(d + 1) * P], prob_t[:, j, :],
                                              start=(j == 0), stop=(j == TT - 1))
                    mm.then_inc(pv_ready, 1)

            low_reg = pe.alloc_register("low_parts")
            pe.wait_ge(ident_ok, 1)
            transposes(0)
            pe.wait_ge(wlo_ok, NF)
            queries_keys(0)
            pe.wait_ge(qk_ok, 4)
            values(0)
            with pe.Fori(0, B - 1) as b:
                scores(b)
                pe.wait_ge(v_ok, b * TT + TT)
                transposes(b + 1)
                queries_keys(b + 1)
                pe.wait_ge(qk_ok, b * 4 + 8)
                attend(b)
                values(b + 1)
                pe.wait_ge(attn_ok, b * DT + DT)
            scores(B - 1)
            attend(B - 1)

            def parts_made(n):
                pe.wait_ge(wlo_ok, parts(n + (QKV_B + 1)))
                pe.wait_ge(has_lo_ok, n + 1)

            def by_low_parts(par, body):
                pe.reg_load(low_reg, has_lo[0:1, par:par + 1].bitcast(I32))
                with pe.If_ne(low_reg, 0):
                    body(True)
                with pe.Else():
                    body(False)

            def gate_up_job(dst, par, g, c, low, following=None):
                for k in range(KT):
                    nc.tensor.matmul(dst, gu_hi[:, par, g, k, :], xn[:, c, 0, k, :], start=(k == 0), stop=False)
                    if low:
                        nc.tensor.matmul(dst, gu_lo[:, par, g, k, :], xn[:, c, 0, k, :], start=False, stop=False)
                    if k == KT - 1 and following is not None:
                        parts_made(following)
                    mm = nc.tensor.matmul(dst, gu_hi[:, par, g, k, :], xn[:, c, 1, k, :],
                                          start=False, stop=(k == KT - 1))
                return mm

            def gate_up(t, par, first=False):
                def jobs(low):
                    for c in range(B):
                        if not first:
                            pe.wait_ge(inter_ok, B * t + (c + 1 - B))
                        gate_up_job(ps[:, 2 * c, :], par, 0, c, low)
                        gate_up_job(ps[:, 2 * c + 1, :], par, 1, c, low,
                                    t + 1 if c == B - 1 else None).then_inc(gu_ready, 1)

                by_low_parts(par, jobs)

            pe.wait_ge(attn_ok, B * DT)
            parts_made(0)
            gate_up(0, 0, first=True)
            with pe.Fori(0, (NI - 1) // 2) as pair:
                t = pair * 2 + 1
                gate_up(t, 1)
                gate_up(t + 1, 0)

            def last_jobs(low):
                for c in range(B):
                    pe.wait_ge(inter_ok, B * NI + (c + 1 - B))
                    gate_up_job(ps[:, 2 * c, :], 1, 0, c, low,
                                IT if c == B - 1 else None).then_inc(gu_ready, 1)

            by_low_parts(1, last_jobs)

            def down(h, par, wo_loads, first=False, last=False):
                def jobs(low):
                    for c in range(B):
                        dst = ps[:, 2 * c, :]
                        if first:
                            pe.wait_ge(q_ok, B * NI + (c + 1))
                        else:
                            pe.wait_ge(res_ok, B * h + (c + 1 - B))
                            pe.wait_ge(sgn_ok, B * h + (JOBS_B + c + 1 - B))
                        for i in range(IT):
                            n = P if i < NI else HALF
                            q = act_q[0:n, i, c * CH:(c + 1) * CH]
                            nc.tensor.matmul(dst, dn_hi[par][0:n, i, :], q,
                                             start=(i == 0), stop=(i == IT - 1 and not low))
                            if low:
                                nc.tensor.matmul(dst, dn_lo[par][0:n, i, :], q, start=False, stop=(i == IT - 1))
                        if c == 0:
                            pe.wait_ge(wo_in_ok[par], wo_loads)
                        for d in range(DT):
                            if c == B - 1 and d == DT - 1 and not last:
                                parts_made(h + (IT + 1))
                            mm = nc.tensor.matmul(ps[:, 2 * c + 1, :], wo_in[:, par, d, :],
                                                  attn_t[:, d, c * CH:(c + 1) * CH],
                                                  start=(d == 0), stop=(d == DT - 1))
                        mm.then_inc(dn_ready, 1)

                by_low_parts(par, jobs)

            down(0, 0, 16, first=True)
            with pe.Fori(0, (HT - 2) // 2) as pair:
                h = pair * 2 + 1
                down(h, 1, 16 * pair + 16)
                down(h + 1, 0, 16 * pair + 32)
            down(HT - 1, 1, 16 * HT // 2, last=True)

        @block.vector
        def _(dve):
            def block_max(blk, src, loaded, count):
                dve.wait_ge(loaded, count)
                nc.vector.tensor_reduce(wmax[:, :], src, AX_X, ALU.max, apply_absolute_value=True).then_inc(wmax_ok, 1)

            def block_scales(blk, par, one, to_value0, to_value1):
                dve.wait_ge(gmax_ok, blk + 1)
                if one:
                    nc.vector.scalar_tensor_tensor(wtop[:, 0:1], gmax[:, 0:1], TINY, gmax[:, 1:2],
                                                   ALU.max, ALU.max)
                    nc.vector.scalar_tensor_tensor(wtop[:, 1:2], gmax[:, 0:1], TINY, gmax[:, 1:2],
                                                   ALU.max, ALU.max).then_inc(wtop_ok, 1)
                else:
                    nc.vector.tensor_scalar(wtop[:, :], gmax[:, :], TINY, None, ALU.max).then_inc(wtop_ok, 1)
                dve.wait_ge(wtop_ok, blk + 1)
                nc.vector.reciprocal(winv[:, :], wtop[:, :]).then_inc(winv_ok, 1)
                nc.vector.tensor_scalar(unit[:, par, :], wtop[:, :], 1.0 / W_UNIT, None, ALU.mult)
                nc.vector.tensor_scalar(descale[:, par, 0:1], wtop[:, 0:1], to_value0, None, ALU.mult)
                nc.vector.tensor_scalar(descale[:, par, 1:2], wtop[:, 1:2], to_value1, None, ALU.mult)
                dve.wait_ge(winv_ok, blk + 1)
                nc.vector.tensor_scalar(to_unit[:, par, :], winv[:, :], W_UNIT, None, ALU.mult)
                nc.vector.tensor_scalar(to_unit_n[:, par, :], winv[:, :], -W_UNIT, None, ALU.mult).then_inc(scales_ok, 1)

            def part_error(done, hi, scale, w):
                dve.wait_ge(whi_ok, done)
                nc.vector.scalar_tensor_tensor(w, hi, scale, w, ALU.mult, ALU.subtract).then_inc(werr_ok, 1)

            GU_VALUE = 1.0 / (W_UNIT * X_UNIT * ACT_Q)
            DN_VALUE = ACT_Q / W_UNIT

            def gu_errors(t, par):
                for g in range(2):
                    part_error(parts(t + QKV_B) + (g + 1),
                               gu_hi[:, par, g, :, :].rearrange("p k c -> p (k c)"),
                               unit[:, par, g:g + 1], gu_in[:, g, :])

            def gu_last_views(g):
                return (gu_hi[:, 1, 0, :, g * HALF:(g + 1) * HALF],
                        gu_in[:, 0, g * GU // 2:(g + 1) * GU // 2].rearrange("p (k c) -> p k c", k=KT))

            def normalise(b, bi):
                for t in range(TT):
                    if t % 2 == 0:
                        dve.wait_ge(x_in_ok[t // 2], 16 * b + 16)
                    for i in range(2):
                        st = nc.vector.bn_stats(stats[:, t, i, :], x_in[:, t, i * CH:(i + 1) * CH])
                    st.then_inc(stats_ok, 1)
                dve.wait_ge(stats_ok, b * TT + TT)
                nc.vector.memset(fence[:, :], 0.0)
                for t in range(TT):
                    ag = nc.vector.bn_aggr(mean_var[:, t, :], stats[:, t, :, :].rearrange("p i s -> p (i s)"))
                ag.then_inc(mv_ok, 1)
                dve.wait_ge(std_ok, b + 1)
                nc.vector.reciprocal(rstd[:, :], std[:, :]).then_inc(rstd_ok, 1)
                dve.wait_ge(rstd_ok, b + 1)
                nc.vector.tensor_scalar(rstd_x[:, :], rstd[:, :], X_UNIT, None, ALU.mult).then_inc(rstd_x_ok, 1)
                dve.wait_ge(rstd_x_ok, b + 1)
                for t in range(TT):
                    nc.vector.tensor_scalar(x_in[:, t, :], x_in[:, t, :], mean_var[:, t, 0:1], rstd_x[:, t:t + 1],
                                            ALU.subtract, ALU.mult).then_inc(norm_ok, 1)

            def x_low(b):
                for t in range(TT):
                    dve.wait_ge(xhi_ok, b * TT + (t + 1))
                    src = ps[:, 2 * (t % 2):2 * (t % 2) + 2, :].rearrange("p a (k s) -> p (a k) s", s=P)
                    dst = xn[:, bass.ds(b, 1), :, :, t * P:(t + 1) * P].rearrange("p a l k s -> p (a l) k s")
                    nc.vector.tensor_tensor(dst[:, 1], src, dst[:, 0], ALU.subtract).then_inc(xlo_ok, 1)

            def soft_max(b):
                for t in range(TT):
                    dve.wait_ge(s_ready, b * TT + (t + 1))
                    mx = nc.vector.tensor_reduce(neg_max[:, t:t + 1], ps[:, 4 + t, :], AX_X, ALU.max, negate=True)
                mx.then_inc(max_ok, 1)
                dve.wait_ge(max_ok, b + 1)
                nc.vector.tensor_scalar(soft_bias[:, :], neg_max[:, :], SOFT, None, ALU.mult).then_inc(bias_ok, 1)

            def soft_normalise(b):
                dve.wait_ge(exp_ok, b * TT + TT)
                nc.vector.reciprocal(row_inv[:, :], row_sum[:, :]).then_inc(inv_ok, 1)
                dve.wait_ge(inv_ok, b + 1)
                for t in range(TT):
                    nc.vector.tensor_scalar(prob[:, t, :], prob[:, t, :], row_inv[:, t:t + 1], None,
                                            ALU.mult).then_inc(prob_ok, 1)

            def copy_v(b):
                for t in range(TT):
                    if t % 2 == 0:
                        dve.wait_ge(v_ready, b * (TT // 2) + (t // 2 + 1))
                    nc.vector.scalar_tensor_tensor(v[:, t, :], ps[:, 2 + t // 2, (t % 2) * D:(t % 2 + 1) * D],
                                                   descale[:, 1, 1:2], bv, ALU.mult, ALU.add).then_inc(v_ok, 1)

            normalise(0, 0)
            block_max(0, wqkv_in.rearrange("p (g n) -> p g n", g=2), wqkv_in_ok, 16)
            block_scales(0, 1, False, 1.0 / (W_UNIT * X_UNIT), 1.0 / (W_UNIT * X_UNIT))
            x_low(0)
            for f in range(NF):
                g = f // (NF // 2)
                part_error(f + 1, wqkv_hi[:, f, :, :].rearrange("p k c -> p (k c)"), unit[:, 1, g:g + 1],
                           wqkv_in[:, f * GU:(f + 1) * GU])
            dve.wait_ge(small_in, 48)
            copy_v(0)
            with dve.Fori(0, B - 1) as b:
                normalise(b + 1, b)
                soft_max(b)
                x_low(b + 1)
                soft_normalise(b)
                copy_v(b + 1)
            soft_max(B - 1)
            block_max(1, gu_in[:, :, :], gu_in_ok, 16)
            soft_normalise(B - 1)
            block_scales(1, 0, False, GU_VALUE, GU_VALUE * ACT_Q)
            gu_errors(0, 0)

            def quantise(j, buf, dst):
                n = dst.shape[0]
                dve.wait_ge(mag_ok, j + 1)
                nc.vector.tensor_scalar(rnd[0:n], mag[0:n, buf, :], HALVES_UP, HALVES,
                                        ALU.add, ALU.max).then_inc(rnd_ok, 1)
                dve.wait_ge(rnd_ok, j + 1)
                nc.vector.tensor_scalar(tmp[0:n], rnd[0:n], HALVES_DOWN, ONES,
                                        ALU.subtract, ALU.add).then_inc(floor_ok, 1)
                dve.wait_ge(floor_ok, j + 1)
                dve.wait_ge(sgn_ok, j + 1)
                nc.vector.scalar_tensor_tensor(sgn[0:n, buf, :], tmp[0:n], ONES_DOWN, sgn[0:n, buf, :],
                                               ALU.subtract, ALU.mult).then_inc(signed_ok, 1)
                dve.wait_ge(signed_ok, j + 1)
                nc.vector.tensor_scalar(dst, sgn[0:n, buf, :], 127.0, -128.0, ALU.min, ALU.max).then_inc(q_ok, 1)

            def job_b(t, par, c):
                buf = c % 2
                j = B * t + c
                dve.wait_ge(silu_ok, j + 1)
                nc.vector.scalar_tensor_tensor(sig[:, buf, :], ps[:, 2 * c + 1, :], descale[:, par, 1:2],
                                               sig[:, buf, :], ALU.mult, ALU.mult).then_inc(inter_ok, 1)
                dst = act_q[:, bass.ds(t, 1), c * CH:(c + 1) * CH].rearrange("p a s -> p (a s)")
                quantise(j, buf, dst)

            def tile_b(t, par, last=False):
                if not last:
                    block_max(t + (QKV_B + 1), gu_in[:, :, :], gu_in_ok, 16 * t + 32)
                job_b(t, par, 0)
                block_scales(t + (QKV_B + 1), 1 - par, False, GU_VALUE, GU_VALUE * ACT_Q)
                gu_errors(t + 1, 1 - par)
                for c in range(1, B):
                    job_b(t, par, c)

            tile_b(0, 0)
            with dve.Fori(0, (NI - 1 - 1) // 2) as pair:
                t = pair * 2 + 1
                tile_b(t, 1)
                tile_b(t + 1, 0)
            tile_b(NI - 2, 1)
            block_max(NI + QKV_B, gu_in[:, 0, :].rearrange("p (g n) -> p g n", g=2), gu_in_ok, 16 * IT)
            job_b(NI - 1, 0, 0)
            block_scales(NI + QKV_B, 1, False, GU_VALUE, GU_VALUE * ACT_Q)
            for g in range(2):
                hi, w = gu_last_views(g)
                part_error(parts(NI + QKV_B) + (g + 1), hi, unit[:, 1, g:g + 1], w)
            for c in range(1, B):
                job_b(NI - 1, 0, c)

            def dn_max(h, count):
                block_max(h + DN_B, dn_in.rearrange("p (g n) -> p g n", g=2), dn_in_ok, count)

            def dn_errors(h, par):
                n = DN // 2
                for g in range(2):
                    part_error(parts(h + DN_B) + (g + 1),
                               dn_hi[par].rearrange("p i c -> p (i c)")[:, g * n:(g + 1) * n],
                               unit[:, par, 0:1], dn_in[:, g * n:(g + 1) * n])

            for c in range(B):
                buf, j = c % 2, B * NI + c
                dve.wait_ge(silu_ok, j + 1)
                nc.vector.tensor_tensor(sig[0:HALF, buf, :], sig[0:HALF, buf, :], mag[0:HALF, buf, :],
                                        ALU.mult).then_inc(inter_ok, 1)
                quantise(j, buf, act_q[0:HALF, NI, c * CH:(c + 1) * CH])
                if c == 0:
                    dn_max(0, 16)
                    block_scales(DN_B, 0, True, DN_VALUE, DN_VALUE)
                    dve.wait_ge(gu_ready, B * NI + 2)
                if c == 1:
                    dn_errors(0, 0)

            def job_c(h, par, c):
                buf = c % 2
                j = B * h + (JOBS_B + c)
                res = out_sb[par][:, c * CH:(c + 1) * CH]
                dve.wait_ge(dn_ready, B * h + (c + 1))
                nc.vector.scalar_tensor_tensor(res, ps[:, 2 * c + 1, :], bo_now[:, par:par + 1],
                                               xf_in[par][:, c * CH:(c + 1) * CH], ALU.add, ALU.add).then_inc(res_ok, 1)
                quantise(j, buf, sgn[:, buf, :])
                dve.wait_ge(q_ok, j + 1)
                dve.wait_ge(res_ok, B * h + (c + 1))
                nc.vector.tensor_tensor(res, res, sgn[:, buf, :], ALU.add).then_inc(out_ok, 1)

            def tile_c(h, par, loads, first=False, last=False):
                if not first:
                    pass
                nc.vector.tensor_copy(bo_now[:, par:par + 1], bo[:, bass.ds(h, 1)]).then_inc(bo_ok, 1)
                dve.wait_ge(bo_ok, h + 1)
                dve.wait_ge(xf_in_ok[par], loads)
                if not last:
                    dn_max(h + 1, 16 * h + 32)
                if first is False:
                    dve.wait_ge(stored[par], store_count[0])
                job_c(h, par, 0)
                if not last:
                    block_scales(h + (DN_B + 1), 1 - par, True, DN_VALUE, DN_VALUE)
                    dn_errors(h + 1, 1 - par)
                for c in range(1, B):
                    job_c(h, par, c)

            store_count = [0]
            tile_c(0, 0, 16, first=True)
            tile_c(1, 1, 16, first=True)
            with dve.Fori(0, (HT - 2 - 2) // 2) as pair:
                h = pair * 2 + 2
                store_count[0] = h * (16 * B // 2)
                tile_c(h, 0, 8 * h + 16)
                tile_c(h + 1, 1, 8 * h + 16)
            store_count[0] = 16 * B * (HT // 2 - 1)
            tile_c(HT - 2, 0, 16 * HT // 2)
            tile_c(HT - 1, 1, 16 * HT // 2, last=True)

        @block.scalar
        def _(act):
            def std_devs(b):
                act.wait_ge(mv_ok, b + 1)
                nc.scalar.activation(std[:, :], mean_var[:, :, 1], ACT.Sqrt, bias=eps[:, 0:1]).then_inc(std_ok, 1)

            def x_high(b):
                for t in range(TT):
                    act.wait_ge(xt_ready, b * TT + (t + 1))
                    src = ps[:, 2 * (t % 2):2 * (t % 2) + 2, :].rearrange("p a (k s) -> p (a k) s", s=P)
                    dst = xn[:, bass.ds(b, 1), :, :, t * P:(t + 1) * P].rearrange("p a l k s -> p (a l) k s")
                    nc.scalar.activation(dst[:, 0], src, ACT.Copy).then_inc(xhi_ok, 1)

            def high(w, scale, hi):
                nc.scalar.activation(hi, w, ACT.Copy, scale=scale).then_inc(whi_ok, 1)

            def low(done, err, scale, lo, total=None):
                act.wait_ge(werr_ok, done)
                nc.scalar.activation(lo, err, ACT.Copy, scale=scale).then_inc(wlo_ok, 1)
                if total is not None:
                    nc.scalar.activation(err, err, ACT.Abs, scale=scale, accum_out=total).then_inc(lo_sum_ok, 1)

            def flat(a, n):
                return a.rearrange("p k c -> p (k c)")

            def copy_qk(b):
                for f in range(2 * DT):
                    act.wait_ge(qk_ready, b * 4 + (f + 1))
                    dst = (q_t if f < DT else k_t)[:, f % DT, :]
                    g = f // (NF // 2)
                    nc.scalar.activation(dst, ps[:, f, :], ACT.Identity, bias=bqk[:, f:f + 1],
                                         scale=descale[:, 1, g:g + 1]).then_inc(qk_ok, 1)

            def exps(b):
                act.wait_ge(bias_ok, b + 1)
                for t in range(TT):
                    nc.scalar.activation(prob[:, t, :], ps[:, 4 + t, :], ACT.Exp, bias=soft_bias[:, t:t + 1],
                                         scale=SOFT, accum_out=row_sum[:, t:t + 1]).then_inc(exp_ok, 1)

            def copy_prob_t(b):
                for t in range(TT):
                    act.wait_ge(pt_ready, b * TT + (t + 1))
                    nc.scalar.activation(prob_t[:, :, t * P:(t + 1) * P],
                                         ps[:, 4 + t, :].rearrange("p (j s) -> p j s", s=P),
                                         ACT.Copy).then_inc(pt_ok, 1)

            def copy_attn(b):
                for d in range(DT):
                    act.wait_ge(pv_ready, b * DT + (d + 1))
                    nc.scalar.activation(attn_t[:, d, bass.ds(b * CH, CH)], ps[:, d, :], ACT.Copy).then_inc(attn_ok, 1)

            def gu_high(t, par):
                act.wait_ge(scales_ok, t + (QKV_B + 1))
                for g in range(2):
                    high(gu_in[:, g, :], to_unit[:, par, g:g + 1], flat(gu_hi[:, par, g, :, :], 0))

            def gu_low(t, par):
                for g in range(2):
                    low(parts(t + QKV_B) + (g + 1), gu_in[:, g, :], to_unit_n[:, par, g:g + 1],
                        flat(gu_lo[:, par, g, :, :], 0), lo_sum[:, par, g:g + 1])

            act.wait_ge(eps_ok, 1)
            std_devs(0)
            x_high(0)
            act.wait_ge(scales_ok, 1)
            for f in range(NF):
                g = f // (NF // 2)
                high(wqkv_in[:, f * GU:(f + 1) * GU], to_unit[:, 1, g:g + 1], flat(wqkv_hi[:, f, :, :], 0))
            for f in range(NF):
                g = f // (NF // 2)
                low(f + 1, wqkv_in[:, f * GU:(f + 1) * GU], to_unit_n[:, 1, g:g + 1], flat(wqkv_lo[:, f, :, :], 0))
            act.wait_ge(small_in, 48)
            copy_qk(0)
            with act.Fori(0, B - 1) as b:
                std_devs(b + 1)
                exps(b)
                x_high(b + 1)
                copy_qk(b + 1)
                copy_prob_t(b)
                copy_attn(b)
            exps(B - 1)
            gu_high(0, 0)
            copy_prob_t(B - 1)
            gu_low(0, 0)
            copy_attn(B - 1)

            def magnitude_sign(j, buf, n, src, scale, used, count):
                nonfirst = not (isinstance(j, int) and j < 2)
                if nonfirst:
                    act.wait_ge(rnd_ok, j - 1)
                nc.scalar.activation(mag[0:n, buf, :], src, ACT.Abs, scale=scale).then_inc(mag_ok, 1)
                if nonfirst:
                    act.wait_ge(used, count)
                nc.scalar.activation(sgn[0:n, buf, :], src, ACT.Sign, scale=scale).then_inc(sgn_ok, 1)

            def job_b(t, par, c):
                buf, j = c % 2, B * t + c
                act.wait_ge(gu_ready, j + 1)
                nc.scalar.activation(sig[:, buf, :], ps[:, 2 * c, :], ACT.Silu,
                                     scale=descale[:, par, 0:1]).then_inc(silu_ok, 1)
                act.wait_ge(inter_ok, j + 1)
                magnitude_sign(j, buf, P, sig[:, buf, :], 1.0, q_ok, j - 1)

            def tile_b(t, par):
                job_b(t, par, 0)
                gu_high(t + 1, 1 - par)
                gu_low(t + 1, 1 - par)
                for c in range(1, B):
                    job_b(t, par, c)

            tile_b(0, 0)
            with act.Fori(0, (NI - 1 - 1) // 2) as pair:
                t = pair * 2 + 1
                tile_b(t, 1)
                tile_b(t + 1, 0)
            tile_b(NI - 2, 1)
            job_b(NI - 1, 0, 0)

            def last_views(g, parts_of):
                return (gu_in[:, 0, g * GU // 2:(g + 1) * GU // 2].rearrange("p (k c) -> p k c", k=KT),
                        parts_of[:, 1, 0, :, g * HALF:(g + 1) * HALF])

            act.wait_ge(scales_ok, NI + QKV_B + 1)
            for g in range(2):
                w, hi = last_views(g, gu_hi)
                high(w, to_unit[:, 1, g:g + 1], hi)
            for g in range(2):
                w, lo = last_views(g, gu_lo)
                low(parts(NI + QKV_B) + (g + 1), w, to_unit_n[:, 1, g:g + 1], lo, lo_sum[:, 1, g:g + 1])
            for c in range(1, B):
                job_b(NI - 1, 0, c)

            def dn_views(par, g, dst):
                n = DN // 2
                return (dn_in[:, g * n:(g + 1) * n], dst[par].rearrange("p i c -> p (i c)")[:, g * n:(g + 1) * n])

            def dn_high(h, par):
                act.wait_ge(scales_ok, h + (DN_B + 1))
                for g in range(2):
                    w, hi = dn_views(par, g, dn_hi)
                    high(w, to_unit[:, par, 0:1], hi)

            def dn_low(h, par):
                for g in range(2):
                    w, lo = dn_views(par, g, dn_lo)
                    low(parts(h + DN_B) + (g + 1), w, to_unit_n[:, par, 0:1], lo, lo_sum[:, par, g:g + 1])

            for c in range(B):
                buf, j = c % 2, B * NI + c
                act.wait_ge(gu_ready, j + 1)
                nc.scalar.activation(sig[0:HALF, buf, :], ps[0:HALF, 2 * c, :], ACT.Silu,
                                     scale=descale[0:HALF, 1, 0:1])
                act.wait_ge(rnd_ok, j - 1)
                nc.scalar.activation(mag[0:HALF, buf, :], ps[HALF:P, 2 * c, :], ACT.Copy,
                                     scale=descale[HALF:P, 1, 1:2]).then_inc(silu_ok, 1)
                act.wait_ge(inter_ok, j + 1)
                magnitude_sign(j, buf, HALF, sig[0:HALF, buf, :], 1.0, q_ok, j - 1)
                if c == 1:
                    dn_high(0, 0)
                if c == 2:
                    dn_low(0, 0)

            def job_c(h, par, c):
                buf = c % 2
                j = B * h + (JOBS_B + c)
                act.wait_ge(dn_ready, B * h + (c + 1))
                if isinstance(h, int) and B * h + c < 2:
                    used, count = q_ok, JOBS_B + c - 1
                else:
                    used, count = out_ok, B * h + (c - 1)
                magnitude_sign(j, buf, P, ps[:, 2 * c, :], descale[:, par, 0:1], used, count)

            def tile_c(h, par, last=False):
                job_c(h, par, 0)
                if not last:
                    dn_high(h + 1, 1 - par)
                    dn_low(h + 1, 1 - par)
                for c in range(1, B):
                    job_c(h, par, c)

            tile_c(0, 0)
            with act.Fori(0, (HT - 1 - 1) // 2) as pair:
                h = pair * 2 + 1
                tile_c(h, 1)
                tile_c(h + 1, 0)
            tile_c(HT - 1, 1, last=True)


def kernel(L0_attn_x, L0_attn_Wqkv, L0_attn_bqkv, L0_attn_Wo, L0_attn_bo, L0_ffn_w_gate, L0_ffn_w_up, L0_ffn_w_down):
    import concourse.bacc as bacc
    import numpy as np
    from concourse.bass_utils import run_bass_kernel_spmd

    batch, seq, hid = L0_attn_x.shape
    kt = hid // P
    nf = L0_attn_Wqkv.shape[1] // P
    inner = L0_ffn_w_gate.shape[0]
    ni, half = inner // P, P // 2
    x = np.asarray(L0_attn_x).reshape(batch * seq, hid)
    wqkv = np.asarray(L0_attn_Wqkv).reshape(kt, P, nf, P).transpose(1, 2, 0, 3).reshape(P, nf, kt * P)
    bqkv = np.asarray(L0_attn_bqkv)
    nqk = nf // 3 * 2

    def tiles(w, n):
        return w.reshape(-1, n, kt, P).transpose(0, 3, 2, 1)

    gate, up, down = (np.asarray(w) for w in (L0_ffn_w_gate, L0_ffn_w_up, L0_ffn_w_down))
    w_gu = np.stack([tiles(w[:ni * P], P).reshape(ni, P, kt * P) for w in (gate, up)], axis=2)
    w_gu_last = np.stack([tiles(w[ni * P:], half)[0].reshape(P, kt * half) for w in (gate, up)], axis=1)
    padded = np.zeros((hid, (ni + 1) * P), down.dtype)
    padded[:, :inner] = down
    w_down = padded.reshape(kt, P, ni + 1, P).transpose(0, 3, 2, 1).reshape(kt, P, (ni + 1) * P)
    wo = np.asarray(L0_attn_Wo).reshape(nf // 3, P, kt, P).transpose(2, 1, 0, 3)
    arrays = {
        "x_tok": x,
        "x_feat": x.T.reshape(kt, P, batch * seq),
        "w_qkv": wqkv,
        "b_qk": bqkv[:nqk * P].reshape(nqk, P).T,
        "b_v": bqkv[nqk * P:],
        "w_gu": w_gu,
        "w_gu_last": w_gu_last.reshape(P, kt * P),
        "w_down": w_down,
        "w_o": wo,
        "b_o": np.asarray(L0_attn_bo).reshape(kt, P).T,
    }
    arrays = {k: np.ascontiguousarray(a) for k, a in arrays.items()}
    nc = bacc.Bacc("TRN2", target_bir_lowering=False, num_devices=1)
    args = [nc.dram_tensor(k, a.shape, mybir.dt.from_np(a.dtype), kind="ExternalInput").ap() for k, a in arrays.items()]
    out = nc.dram_tensor("out", (kt, P, batch * seq), F32, kind="ExternalOutput").ap()
    build(nc, *args, out)
    r = run_bass_kernel_spmd(nc, [arrays], core_ids=[0])
    return r.results[0]["out"].reshape(hid, batch, seq).transpose(1, 2, 0)
```

```python
from contextlib import ExitStack

import concourse.bass as bass
from concourse import mybir

ALU = mybir.AluOpType
ACT = mybir.ActivationFunctionType
F32 = mybir.dt.float32
F16 = mybir.dt.float16
I32 = mybir.dt.int32
AX_X = mybir.AxisListType.X
ABSMAX = bass.bass_isa.ReduceOp.absmax

P = 128
W_UNIT = 8192.0
X_UNIT = 1024.0
HALVES = 2.0 ** 22
HALVES_UP = HALVES - 0.25
HALVES_DOWN = HALVES - 0.75
ONES = 2.0 ** 23
ONES_DOWN = 2.0 ** 23 + 1
TINY = 1e-30
EPS = 1e-5
ACT_Q = 128.0


def build(nc, x_tok, x_feat, w_qkv, b_qk, b_v, w_gu, w_gu_last, w_down, w_o, b_o, out):
    TOK, H = x_tok.shape
    KT = H // P
    CH = 512
    B = TOK // CH
    TT = CH // P
    NF = w_qkv.shape[1]
    QKV = 3
    DT = NF // QKV
    D = DT * P
    NI = w_gu.shape[0]
    HALF = P // 2
    IT = NI + 1
    HT = H // P
    SOFT = float(D) ** -0.5
    GU = KT * P
    DN = IT * P

    with ExitStack() as ctx:
        def sb(name, shape, dt):
            return ctx.enter_context(nc.sbuf_tensor(name, shape, dt))

        def sem(name):
            return ctx.enter_context(nc.semaphore(name))

        xn = sb("xn", [P, B, 2, KT, CH], F16)
        act_q = sb("act_q", [P, IT, TOK], F16)
        attn_t = sb("attn_t", [P, DT, TOK], F32)
        gu_in = sb("gu_in", [P, 2, GU], F32)
        gu_hi = sb("gu_hi", [P, 2, 2, KT, P], F16)
        gu_lo = sb("gu_lo", [P, 2, 2, KT, P], F16)
        sig = sb("sig", [P, 2, CH], F32)
        mag = sb("mag", [P, 2, CH], F32)
        sgn = sb("sgn", [P, 2, CH], F16)
        rnd = sb("rnd", [P, CH], F32)
        tmp = sb("tmp", [P, CH], F32)
        ident = sb("ident", [P, P], F32)
        eps = sb("eps", [P, 1], F32)
        bqk = sb("bqk", [P, 2 * DT], F32)
        bo = sb("bo", [P, HT], F32)
        wmax = sb("wmax", [P, 2, 2], F32)
        gmax = sb("gmax", [P, 2, 2], F32)
        wtop = sb("wtop", [P, 2], F32)
        winv = sb("winv", [P, 2], F32)
        to_unit = sb("to_unit", [P, 2 + QKV, 2], F32)
        to_unit_n = sb("to_unit_n", [P, 2 + QKV, 2], F32)
        unit = sb("unit", [P, 2 + QKV, 2], F32)
        descale = sb("descale", [P, 2 + QKV, 2], F32)
        lo_sum = sb("lo_sum", [P, 2, 2], F32)
        lo_top = sb("lo_top", [P, 2], F32)
        has_lo = sb("has_lo", [P, 2], F32)
        stats = sb("stats", [P, TT, 2, 6], F32)
        mean_var = sb("mean_var", [P, TT, 2], F32)
        std = sb("std", [P, TT], F32)
        rstd = sb("rstd", [P, TT], F32)
        rstd_x = sb("rstd_x", [P, TT], F32)
        neg_max = sb("neg_max", [P, TT], F32)
        soft_bias = sb("soft_bias", [P, TT], F32)
        row_sum = sb("row_sum", [P, TT], F32)
        row_inv = sb("row_inv", [P, TT], F32)
        fence = sb("fence", [P, 1], F32)
        bo_now = sb("bo_now", [P, 2], F32)

        a32 = act_q[:, :, :].rearrange("p a b -> p (a b)").bitcast(F32)
        place = [0]

        def in_a(n):
            place[0] += n
            assert place[0] <= IT * TOK // 2
            return a32[:, place[0] - n:place[0]]

        wqkv_in = in_a(NF * GU)
        wqkv_hi = in_a(NF * GU // 2).bitcast(F16).rearrange("p (f k c) -> p f k c", f=NF, k=KT)
        wqkv_lo = in_a(NF * GU // 2).bitcast(F16).rearrange("p (f k c) -> p f k c", f=NF, k=KT)
        x_in = in_a(TT * H).rearrange("p (t h) -> p t h", t=TT)
        q_t = in_a(DT * CH).rearrange("p (d s) -> p d s", d=DT)
        k_t = in_a(DT * CH).rearrange("p (d s) -> p d s", d=DT)
        v = in_a(TT * D).rearrange("p (t d) -> p t d", t=TT)
        bv = in_a(D)
        prob = wqkv_in[:, 0:TT * CH].rearrange("p (t s) -> p t s", t=TT)
        prob_t = wqkv_in[:, TT * CH:2 * TT * CH].rearrange("p (t s) -> p t s", t=TT)

        def in_xn(b):
            return xn[:, b, :, :, :].rearrange("p a k s -> p (a k s)")

        dn_in = in_xn(0).bitcast(F32)[:, 0:DN]
        wo_in = in_xn(0).bitcast(F32)[:, DN:DN + 2 * DT * P].rearrange("p (b d c) -> p b d c", b=2, d=DT)
        dn_hi = [in_xn(1 + i)[:, 0:DN].rearrange("p (i c) -> p i c", i=IT) for i in range(2)]
        dn_lo = [in_xn(1 + i)[:, DN:2 * DN].rearrange("p (i c) -> p i c", i=IT) for i in range(2)]
        xf_in = [in_xn(3).bitcast(F32)[:, i * TOK:(i + 1) * TOK] for i in range(2)]
        out_sb = [gu_hi[:, :, :, :, :].rearrange("p a b k c -> p (a b k c)").bitcast(F32)[:, 0:TOK],
                  gu_lo[:, :, :, :, :].rearrange("p a b k c -> p (a b k c)").bitcast(F32)[:, 0:TOK]]

        ps = ctx.enter_context(nc.psum_tensor("ps", [P, 8, CH], F32))

        ident0, ident_ok, eps_ok = sem("ident0"), sem("ident_ok"), sem("eps_ok")
        small_in = sem("small_in")
        wqkv_in_ok = [sem(f"wqkv_in_ok{i}") for i in range(QKV)]
        x_in_ok = [sem(f"x_in_ok{i}") for i in range(TT)]
        gu_in_ok, dn_in_ok = sem("gu_in_ok"), sem("dn_in_ok")
        wo_in_ok = [sem(f"wo_in_ok{i}") for i in range(2)]
        xf_in_ok = [sem(f"xf_in_ok{i}") for i in range(2)]
        stored = [sem(f"stored{i}") for i in range(2)]
        wmax_ok, gmax_ok, wtop_ok, winv_ok, scales_ok = (
            sem("wmax_ok"), sem("gmax_ok"), sem("wtop_ok"), sem("winv_ok"), sem("scales_ok"))
        whi_ok, werr_ok, wlo_ok = sem("whi_ok"), sem("werr_ok"), sem("wlo_ok")
        lo_sum_ok, lo_top_ok, has_lo_ok = sem("lo_sum_ok"), sem("lo_top_ok"), sem("has_lo_ok")
        stats_ok, mv_ok, std_ok, rstd_ok, rstd_x_ok, norm_ok = (
            sem("stats_ok"), sem("mv_ok"), sem("std_ok"), sem("rstd_ok"), sem("rstd_x_ok"), sem("norm_ok"))
        xt_ready, xhi_ok, xlo_ok = sem("xt_ready"), sem("xhi_ok"), sem("xlo_ok")
        qk_ready, qk_ok, v_ready, v_ok = sem("qk_ready"), sem("qk_ok"), sem("v_ready"), sem("v_ok")
        s_ready, max_ok, bias_ok, exp_ok = sem("s_ready"), sem("max_ok"), sem("bias_ok"), sem("exp_ok")
        inv_ok, prob_ok, pt_ready, pt_ok = sem("inv_ok"), sem("prob_ok"), sem("pt_ready"), sem("pt_ok")
        pv_ready, attn_ok = sem("pv_ready"), sem("attn_ok")
        gu_ready, silu_ok, inter_ok, mag_ok, sgn_ok = (
            sem("gu_ready"), sem("silu_ok"), sem("inter_ok"), sem("mag_ok"), sem("sgn_ok"))
        rnd_ok, floor_ok, signed_ok, q_ok = sem("rnd_ok"), sem("floor_ok"), sem("signed_ok"), sem("q_ok")
        dn_ready, res_ok, out_ok, bo_ok = sem("dn_ready"), sem("res_ok"), sem("out_ok"), sem("bo_ok")

        JOBS_B = IT * B

        block = ctx.enter_context(nc.Block())

        @block.sync
        def _(sp):
            def load_x(b):
                for t in range(TT):
                    sp.dma_start(x_in[:, t, :], x_tok[bass.ds(b * CH + t * P, P), :]).then_inc(x_in_ok[t], 16)

            load_x(0)
            for i in range(QKV):
                sp.dma_start(wqkv_in[:, 2 * i * GU:2 * (i + 1) * GU],
                             w_qkv[:, 2 * i:2 * i + 2, :].rearrange("p f n -> p (f n)")).then_inc(wqkv_in_ok[i], 16)
            sp.dma_start(bqk[:, :], b_qk).then_inc(small_in, 16)
            sp.dma_start(bo[:, :], b_o).then_inc(small_in, 16)
            sp.dma_start(bv, b_v.partition_broadcast(P)).then_inc(small_in, 16)
            sp.dma_start(gu_in[:, 0, :], w_gu_last).then_inc(gu_in_ok, 16)
            with sp.Fori(1, B) as b:
                sp.wait_ge(xt_ready, b * TT)
                load_x(b)
            with sp.Fori(1, IT) as n:
                sp.wait_ge(lo_sum_ok, 2 * n)
                sp.dma_start(gu_in[:, :, :], w_gu[bass.ds(n - 1, 1)].rearrange("a p g n -> p (a g) n")).then_inc(gu_in_ok, 16)
            sp.wait_ge(gu_ready, NI * B + 1)
            sp.dma_start(dn_in, w_down[0]).then_inc(dn_in_ok, 16)
            sp.dma_start(wo_in[:, 0, :, :], w_o[0]).then_inc(wo_in_ok[0], 16)
            sp.wait_ge(gu_ready, NI * B + B)
            sp.dma_start(xf_in[0], x_feat[0]).then_inc(xf_in_ok[0], 16)

            def load_down(h):
                sp.wait_ge(lo_sum_ok, 2 * h + 2 * IT)
                sp.dma_start(dn_in, w_down[bass.ds(h, 1)].rearrange("a p n -> p (a n)")).then_inc(dn_in_ok, 16)

            def load_rest(h, par):
                sp.dma_start(wo_in[:, par, :, :],
                             w_o[bass.ds(h, 1)].rearrange("a p d c -> p (a d) c")).then_inc(wo_in_ok[par], 16)
                sp.dma_start(xf_in[par], x_feat[bass.ds(h, 1)].rearrange("a p n -> p (a n)")).then_inc(xf_in_ok[par], 16)

            def store(h, par, chunks):
                for c in chunks:
                    sp.wait_ge(out_ok, B * h + (c + 1))
                    sp.dma_start(out[bass.ds(h, 1)].rearrange("a p n -> p (a n)")[:, c * CH:(c + 1) * CH],
                                 out_sb[par][:, c * CH:(c + 1) * CH]).then_inc(stored[par], 16)

            def tile(h, par):
                store(h, par, range(0, 2))
                load_down(h + 2)
                store(h, par, range(2, B))
                load_rest(h + 2, par)

            load_down(1)
            load_rest(1, 1)
            tile(0, 0)
            with sp.Fori(0, (HT - 2) // 2 - 1) as pair:
                tile(pair * 2 + 1, 1)
                tile(pair * 2 + 2, 0)
            tile(HT - 3, 1)
            store(HT - 2, 0, range(B))
            store(HT - 1, 1, range(B))
            for par in range(2):
                sp.wait_ge(stored[par], 16 * B * HT // 2)

        @block.gpsimd
        def _(pool):
            nc.gpsimd.memset(ident[:, :], 0.0).then_inc(ident0, 1)
            nc.gpsimd.memset(eps[:, :], EPS).then_inc(eps_ok, 1)
            pool.wait_ge(ident0, 1)
            nc.gpsimd.affine_select(out=ident[:, :], in_=ident[:, :], compare_op=ALU.not_equal, fill=1.0,
                                    base=0, pattern=[[-1, P]], channel_multiplier=1).then_inc(ident_ok, 1)
            for blk in range(QKV + IT + HT):
                pool.wait_ge(wmax_ok, blk + 1)
                nc.gpsimd.partition_all_reduce(gmax[:, blk % 2, :], wmax[:, blk % 2, :], P, ABSMAX).then_inc(gmax_ok, 1)
                if blk >= QKV:
                    n, par = blk - QKV, (blk - QKV) % 2
                    pool.wait_ge(lo_sum_ok, 2 * n + 2)
                    nc.gpsimd.partition_all_reduce(lo_top[:, :], lo_sum[:, par, :], P, ABSMAX).then_inc(lo_top_ok, 1)
                    pool.wait_ge(lo_top_ok, n + 1)
                    nc.gpsimd.tensor_tensor(has_lo[:, par:par + 1], lo_top[:, 0:1], lo_top[:, 1:2],
                                            ALU.add).then_inc(has_lo_ok, 1)

        @block.tensor
        def _(pe):
            def xpart(b, part, k, lo, n):
                if isinstance(b, int):
                    return xn[:, b, part, k, lo:lo + n]
                return xn[:, bass.ds(b, 1), part, k, lo:lo + n].rearrange("p a s -> p (a s)")

            def transposes(b, tiles):
                for t in tiles:
                    pe.wait_ge(norm_ok, b * TT + (t + 1))
                    if t >= 2:
                        pe.wait_ge(xhi_ok, b * TT + (t - 1))
                        pe.wait_ge(xlo_ok, b * TT + (t - 1))
                    for k in range(KT):
                        mm = nc.tensor.transpose(ps[:, 2 * (t % 2) + k // 4, (k % 4) * P:(k % 4 + 1) * P],
                                                 x_in[:, t, k * P:(k + 1) * P], ident[:, :])
                    mm.then_inc(xt_ready, 1)

            def queries_keys(b, first=False):
                pe.wait_ge(xhi_ok, b * TT + TT)
                pe.wait_ge(xlo_ok, b * TT + TT)
                for f in range(2 * DT):
                    if first and f % DT == 0:
                        pe.wait_ge(wlo_ok, f + 2)
                    for k in range(KT):
                        nc.tensor.matmul(ps[:, f, :], wqkv_hi[:, f, k, :], xpart(b, 0, k, 0, CH),
                                         start=(k == 0), stop=False)
                        nc.tensor.matmul(ps[:, f, :], wqkv_hi[:, f, k, :], xpart(b, 1, k, 0, CH),
                                         start=False, stop=False)
                        mm = nc.tensor.matmul(ps[:, f, :], wqkv_lo[:, f, k, :], xpart(b, 0, k, 0, CH),
                                              start=False, stop=(k == KT - 1))
                    mm.then_inc(qk_ready, 1)

            def values(b):
                for t in range(TT):
                    dst = ps[:, 2 + t // 2, (t % 2) * D:(t % 2 + 1) * D]
                    for k in range(KT):
                        nc.tensor.matmul(dst, xpart(b, 0, k, t * P, P), wqkv_hi[:, 2 * DT:NF, k, :],
                                         start=(k == 0), stop=False)
                        nc.tensor.matmul(dst, xpart(b, 0, k, t * P, P), wqkv_lo[:, 2 * DT:NF, k, :],
                                         start=False, stop=False)
                        mm = nc.tensor.matmul(dst, xpart(b, 1, k, t * P, P), wqkv_hi[:, 2 * DT:NF, k, :],
                                              start=False, stop=(k == KT - 1))
                    if t % 2:
                        mm.then_inc(v_ready, 1)

            def scores(b, tiles):
                for t in tiles:
                    for d in range(DT):
                        mm = nc.tensor.matmul(ps[:, 4 + t, :], q_t[:, d, t * P:(t + 1) * P], k_t[:, d, :],
                                              start=(d == 0), stop=(d == DT - 1))
                    mm.then_inc(s_ready, 1)

            def transpose_probs(b):
                for t in range(TT):
                    pe.wait_ge(prob_ok, b * TT + (t + 1))
                    for j in range(TT):
                        mm = nc.tensor.transpose(ps[:, 4 + t, j * P:(j + 1) * P],
                                                 prob[:, t, j * P:(j + 1) * P], ident[:, :])
                    mm.then_inc(pt_ready, 1)

            def attend(b):
                pe.wait_ge(pt_ok, b * TT + TT)
                for d in range(DT):
                    for j in range(TT):
                        mm = nc.tensor.matmul(ps[:, d, :], v[:, j, d * P:(d + 1) * P], prob_t[:, j, :],
                                              start=(j == 0), stop=(j == TT - 1))
                    mm.then_inc(pv_ready, 1)

            low_reg = pe.alloc_register("low_parts")

            def batch(b):
                transposes(b + 1, range(0, 2))
                scores(b, [1])
                transposes(b + 1, range(2, TT))
                scores(b, range(2, TT))
                queries_keys(b + 1)
                transpose_probs(b)
                pe.wait_ge(qk_ok, b * 4 + 8)
                values(b + 1)
                attend(b)
                scores(b + 1, [0])
                pe.wait_ge(attn_ok, b * DT + DT)
                pe.wait_ge(v_ok, b * TT + 2 * TT)

            pe.wait_ge(ident_ok, 1)
            transposes(0, range(TT))
            queries_keys(0, first=True)
            pe.wait_ge(qk_ok, 4)
            pe.wait_ge(wlo_ok, 2 * QKV)
            values(0)
            scores(0, [0])
            pe.wait_ge(v_ok, TT)
            with pe.Fori(0, B - 2) as b:
                batch(b)
            batch(B - 2)
            scores(B - 1, range(1, TT))

            def parts_made(n):
                pe.wait_ge(wlo_ok, 2 * n + (2 * QKV + 2))
                pe.wait_ge(has_lo_ok, n + 1)

            def by_low_parts(par, body):
                pe.reg_load(low_reg, has_lo[0:1, par:par + 1].bitcast(I32))
                with pe.If_ne(low_reg, 0):
                    body(True)
                with pe.Else():
                    body(False)

            def gate_up_job(dst, par, g, c, low, following=None):
                for k in range(KT):
                    nc.tensor.matmul(dst, gu_hi[:, par, g, k, :], xn[:, c, 0, k, :], start=(k == 0), stop=False)
                    if low:
                        nc.tensor.matmul(dst, gu_lo[:, par, g, k, :], xn[:, c, 0, k, :], start=False, stop=False)
                    if k == KT - 1 and following is not None:
                        parts_made(following)
                    mm = nc.tensor.matmul(dst, gu_hi[:, par, g, k, :], xn[:, c, 1, k, :],
                                          start=False, stop=(k == KT - 1))
                return mm

            def half_block(low):
                for c in range(B):
                    if c >= 2:
                        pe.wait_ge(inter_ok, c - 1)
                    gate_up_job(ps[:, 2 + c % 2, :], 0, 0, c, low, 1 if c == B - 1 else None).then_inc(gu_ready, 1)
                    if c == 1:
                        transpose_probs(B - 1)
                    if c == 2:
                        attend(B - 1)

            parts_made(0)
            by_low_parts(0, half_block)

            def gate_up(n, par, first=False, following=True):
                def jobs(low):
                    for c in range(B):
                        if not first:
                            pe.wait_ge(inter_ok, B * n + (c + 1 - B))
                        elif c == 0:
                            pe.wait_ge(attn_ok, B * DT)
                        elif c == 1:
                            pe.wait_ge(inter_ok, B)
                        gate_up_job(ps[:, 2 * c, :], par, 0, c, low)
                        gate_up_job(ps[:, 2 * c + 1, :], par, 1, c, low,
                                    n + 1 if c == B - 1 and following else None).then_inc(gu_ready, 1)

                by_low_parts(par, jobs)

            gate_up(1, 1, first=True)
            with pe.Fori(1, NI // 2) as pair:
                gate_up(pair * 2, 0)
                gate_up(pair * 2 + 1, 1)
            gate_up(NI - 1, 0)
            gate_up(NI, 1, following=False)

            def project(c, par, following=None):
                for d in range(DT):
                    if d == DT - 1 and following is not None:
                        parts_made(following)
                    mm = nc.tensor.matmul(ps[:, 2 * c + 1, :], wo_in[:, par, d, :], attn_t[:, d, c * CH:(c + 1) * CH],
                                          start=(d == 0), stop=(d == DT - 1))
                return mm

            def down(h, par, wo_loads, first=False, last=False):
                def jobs(low):
                    for c in range(B):
                        dst = ps[:, 2 * c, :]
                        if first:
                            pe.wait_ge(q_ok, B * NI + (c + 1))
                        else:
                            pe.wait_ge(res_ok, B * h + (c + 1 - B))
                            pe.wait_ge(sgn_ok, B * h + (JOBS_B + c + 1 - B))
                        for i in range(IT):
                            n = P if i < NI else HALF
                            q = act_q[0:n, i, c * CH:(c + 1) * CH]
                            if low:
                                nc.tensor.matmul(dst, dn_lo[par][0:n, i, :], q, start=(i == 0), stop=False)
                            if first and c == B - 1 and i == IT - 1:
                                parts_made(h + (IT + 1))
                            mm = nc.tensor.matmul(dst, dn_hi[par][0:n, i, :], q,
                                                  start=(i == 0 and not low), stop=(i == IT - 1))
                        if c == 0 and not first:
                            pe.wait_ge(wo_in_ok[par], wo_loads)
                        if not first:
                            mm = project(c, par, h + (IT + 1) if c == B - 1 and not last else None)
                        mm.then_inc(dn_ready, 1)

                by_low_parts(par, jobs)

            pe.wait_ge(wo_in_ok[0], 16)
            for c in range(B):
                pe.wait_ge(inter_ok, B * NI + (c + 1))
                project(c, 0)
            parts_made(IT)
            down(0, 0, 16, first=True)
            with pe.Fori(0, (HT - 2) // 2) as pair:
                h = pair * 2 + 1
                down(h, 1, 16 * pair + 16)
                down(h + 1, 0, 16 * pair + 32)
            down(HT - 1, 1, 16 * HT // 2, last=True)

        @block.vector
        def _(dve):
            def block_max(blk, par, src, loaded, count):
                dve.wait_ge(loaded, count)
                nc.vector.tensor_reduce(wmax[:, par, :], src, AX_X, ALU.max, apply_absolute_value=True).then_inc(wmax_ok, 1)

            def block_scales(blk, par, place, one, to_value0, to_value1):
                dve.wait_ge(gmax_ok, blk + 1)
                if one:
                    nc.vector.scalar_tensor_tensor(wtop[:, 0:1], gmax[:, par, 0:1], TINY, gmax[:, par, 1:2],
                                                   ALU.max, ALU.max)
                    nc.vector.scalar_tensor_tensor(wtop[:, 1:2], gmax[:, par, 0:1], TINY, gmax[:, par, 1:2],
                                                   ALU.max, ALU.max).then_inc(wtop_ok, 1)
                else:
                    nc.vector.tensor_scalar(wtop[:, :], gmax[:, par, :], TINY, None, ALU.max).then_inc(wtop_ok, 1)
                dve.wait_ge(wtop_ok, blk + 1)
                nc.vector.reciprocal(winv[:, :], wtop[:, :]).then_inc(winv_ok, 1)
                nc.vector.tensor_scalar(unit[:, place, :], wtop[:, :], 1.0 / W_UNIT, None, ALU.mult)
                nc.vector.tensor_scalar(descale[:, place, 0:1], wtop[:, 0:1], to_value0, None, ALU.mult)
                nc.vector.tensor_scalar(descale[:, place, 1:2], wtop[:, 1:2], to_value1, None, ALU.mult)
                dve.wait_ge(winv_ok, blk + 1)
                nc.vector.tensor_scalar(to_unit[:, place, :], winv[:, :], W_UNIT, None, ALU.mult)
                nc.vector.tensor_scalar(to_unit_n[:, place, :], winv[:, :], -W_UNIT, None, ALU.mult).then_inc(scales_ok, 1)

            def part_error(done, hi, scale, w):
                dve.wait_ge(whi_ok, done)
                nc.vector.scalar_tensor_tensor(w, hi, scale, w, ALU.mult, ALU.subtract).then_inc(werr_ok, 1)

            QKV_VALUE = 1.0 / (W_UNIT * X_UNIT)
            GU_VALUE = QKV_VALUE / ACT_Q
            DN_VALUE = ACT_Q / W_UNIT

            def qkv_max(i):
                block_max(i, i % 2, wqkv_in[:, 2 * i * GU:2 * (i + 1) * GU].rearrange("p (g n) -> p g n", g=2),
                          wqkv_in_ok[i], 16)

            def qkv_scales(i):
                block_scales(i, i % 2, 2 + i, True, QKV_VALUE, QKV_VALUE)

            def qkv_errors(i):
                for f in range(2 * i, 2 * i + 2):
                    part_error(f + 1, wqkv_hi[:, f, :, :].rearrange("p k c -> p (k c)"), unit[:, 2 + i, 0:1],
                               wqkv_in[:, f * GU:(f + 1) * GU])

            def gu_max(n, par, half=False):
                src = gu_in[:, 0, :].rearrange("p (g n) -> p g n", g=2) if half else gu_in[:, :, :]
                block_max(n + QKV, 1 - par, src, gu_in_ok, 16 * n + 16)

            def gu_scales(n, par):
                block_scales(n + QKV, 1 - par, par, False, GU_VALUE, GU_VALUE * ACT_Q)

            def gu_errors(n, par, half=False):
                for g in range(2):
                    if half:
                        hi = gu_hi[:, 0, 0, :, g * HALF:(g + 1) * HALF]
                        w = gu_in[:, 0, g * GU // 2:(g + 1) * GU // 2].rearrange("p (k c) -> p k c", k=KT)
                    else:
                        hi = gu_hi[:, par, g, :, :].rearrange("p k c -> p (k c)")
                        w = gu_in[:, g, :]
                    part_error(2 * n + (2 * QKV + g + 1), hi, unit[:, par, g:g + 1], w)

            def normalise(b):
                for t in range(TT):
                    dve.wait_ge(x_in_ok[t], 16 * b + 16)
                    for i in range(2):
                        st = nc.vector.bn_stats(stats[:, t, i, :], x_in[:, t, i * CH:(i + 1) * CH])
                    st.then_inc(stats_ok, 1)
                dve.wait_ge(stats_ok, b * TT + TT)
                nc.vector.memset(fence[:, :], 0.0)
                for t in range(TT):
                    ag = nc.vector.bn_aggr(mean_var[:, t, :], stats[:, t, :, :].rearrange("p i s -> p (i s)"))
                ag.then_inc(mv_ok, 1)
                dve.wait_ge(std_ok, b + 1)
                nc.vector.reciprocal(rstd[:, :], std[:, :]).then_inc(rstd_ok, 1)
                dve.wait_ge(rstd_ok, b + 1)
                nc.vector.tensor_scalar(rstd_x[:, :], rstd[:, :], X_UNIT, None, ALU.mult).then_inc(rstd_x_ok, 1)
                dve.wait_ge(rstd_x_ok, b + 1)
                for t in range(TT):
                    nc.vector.tensor_scalar(x_in[:, t, :], x_in[:, t, :], mean_var[:, t, 0:1], rstd_x[:, t:t + 1],
                                            ALU.subtract, ALU.mult).then_inc(norm_ok, 1)

            def x_low(b, tiles):
                for t in tiles:
                    dve.wait_ge(xhi_ok, b * TT + (t + 1))
                    src = ps[:, 2 * (t % 2):2 * (t % 2) + 2, :].rearrange("p a (k s) -> p (a k) s", s=P)
                    dst = xn[:, bass.ds(b, 1), :, :, t * P:(t + 1) * P].rearrange("p a l k s -> p (a l) k s")
                    nc.vector.tensor_tensor(dst[:, 1], src, dst[:, 0], ALU.subtract).then_inc(xlo_ok, 1)

            def row_maxima(b, tiles):
                for t in tiles:
                    dve.wait_ge(s_ready, b * TT + (t + 1))
                    nc.vector.tensor_reduce(neg_max[:, t:t + 1], ps[:, 4 + t, :], AX_X, ALU.max,
                                            negate=True).then_inc(max_ok, 1)

            def exponent_biases(b):
                dve.wait_ge(max_ok, b * TT + TT)
                nc.vector.tensor_scalar(soft_bias[:, :], neg_max[:, :], SOFT, None, ALU.mult).then_inc(bias_ok, 1)

            def soft_normalise(b):
                dve.wait_ge(exp_ok, b * TT + TT)
                nc.vector.reciprocal(row_inv[:, :], row_sum[:, :]).then_inc(inv_ok, 1)
                dve.wait_ge(inv_ok, b + 1)
                for t in range(TT):
                    nc.vector.tensor_scalar(prob[:, t, :], prob[:, t, :], row_inv[:, t:t + 1], None,
                                            ALU.mult).then_inc(prob_ok, 1)

            def copy_v(b):
                for t in range(TT):
                    if t % 2 == 0:
                        dve.wait_ge(v_ready, b * (TT // 2) + (t // 2 + 1))
                    nc.vector.scalar_tensor_tensor(v[:, t, :], ps[:, 2 + t // 2, (t % 2) * D:(t % 2 + 1) * D],
                                                   descale[:, 4, 0:1], bv, ALU.mult, ALU.add).then_inc(v_ok, 1)

            normalise(0)
            qkv_max(0)
            x_low(0, range(0, 2))
            qkv_scales(0)
            qkv_max(1)
            qkv_errors(0)
            x_low(0, range(2, TT))
            qkv_scales(1)
            qkv_errors(1)
            qkv_max(2)
            qkv_scales(2)
            qkv_errors(2)
            normalise(1)
            dve.wait_ge(small_in, 48)
            copy_v(0)

            def batch(b, more=True):
                row_maxima(b, [0])
                x_low(b + 1, range(0, 2))
                row_maxima(b, [1])
                x_low(b + 1, range(2, TT))
                row_maxima(b, range(2, TT))
                exponent_biases(b)
                soft_normalise(b)
                if more:
                    normalise(b + 2)

            with dve.Fori(0, B - 2) as b:
                batch(b)
                dve.wait_ge(pv_ready, b * DT + DT)
                copy_v(b + 1)
            batch(B - 2, more=False)
            gu_max(0, 0, half=True)
            gu_scales(0, 0)
            gu_errors(0, 0, half=True)
            dve.wait_ge(pv_ready, (B - 1) * DT)
            copy_v(B - 1)
            row_maxima(B - 1, range(TT))
            exponent_biases(B - 1)
            gu_max(1, 1)
            soft_normalise(B - 1)

            def quantise(j, buf, dst):
                n = dst.shape[0]
                dve.wait_ge(mag_ok, j + 1)
                nc.vector.tensor_scalar(rnd[0:n], mag[0:n, buf, :], HALVES_UP, HALVES,
                                        ALU.add, ALU.max).then_inc(rnd_ok, 1)
                dve.wait_ge(rnd_ok, j + 1)
                nc.vector.tensor_scalar(tmp[0:n], rnd[0:n], HALVES_DOWN, ONES,
                                        ALU.subtract, ALU.add).then_inc(floor_ok, 1)
                dve.wait_ge(floor_ok, j + 1)
                dve.wait_ge(sgn_ok, j + 1)
                nc.vector.scalar_tensor_tensor(sgn[0:n, buf, :], tmp[0:n], ONES_DOWN, sgn[0:n, buf, :],
                                               ALU.subtract, ALU.mult).then_inc(signed_ok, 1)
                dve.wait_ge(signed_ok, j + 1)
                nc.vector.tensor_scalar(dst, sgn[0:n, buf, :], 127.0, -128.0, ALU.min, ALU.max).then_inc(q_ok, 1)

            def job_b(n, par, c):
                buf = c % 2
                j = B * n + c
                dve.wait_ge(silu_ok, j + 1)
                nc.vector.scalar_tensor_tensor(sig[:, buf, :], ps[:, 2 * c + 1, :], descale[:, par, 1:2],
                                               sig[:, buf, :], ALU.mult, ALU.mult).then_inc(inter_ok, 1)
                quantise(j, buf, act_q[:, bass.ds(n - 1, 1), c * CH:(c + 1) * CH].rearrange("p a s -> p (a s)"))

            for c in range(B):
                buf, j = c % 2, c
                dve.wait_ge(silu_ok, j + 1)
                nc.vector.tensor_tensor(sig[0:HALF, buf, :], sig[0:HALF, buf, :], mag[0:HALF, buf, :],
                                        ALU.mult).then_inc(inter_ok, 1)
                quantise(j, buf, act_q[0:HALF, NI, c * CH:(c + 1) * CH])
                if c == 0:
                    gu_scales(1, 1)
                    gu_errors(1, 1)
            dve.wait_ge(attn_ok, B * DT)

            def tile_b(n, par):
                gu_max(n + 1, 1 - par)
                job_b(n, par, 0)
                gu_scales(n + 1, 1 - par)
                gu_errors(n + 1, 1 - par)
                for c in range(1, B):
                    job_b(n, par, c)

            with dve.Fori(0, NI // 2) as pair:
                tile_b(pair * 2 + 1, 1)
                tile_b(pair * 2 + 2, 0)

            def dn_max(h, par, count):
                block_max(h + (QKV + IT), 1 - par, dn_in.rearrange("p (g n) -> p g n", g=2), dn_in_ok, count)

            def dn_scales(h, par):
                block_scales(h + (QKV + IT), 1 - par, par, True, DN_VALUE, DN_VALUE)

            def dn_errors(h, par):
                n = DN // 2
                for g in range(2):
                    part_error(2 * h + (2 * (QKV + IT) + g + 1),
                               dn_hi[par].rearrange("p i c -> p (i c)")[:, g * n:(g + 1) * n],
                               unit[:, par, 0:1], dn_in[:, g * n:(g + 1) * n])

            job_b(NI, 1, 0)
            job_b(NI, 1, 1)
            dn_max(0, 0, 16)
            dn_scales(0, 0)
            dn_errors(0, 0)
            job_b(NI, 1, 2)
            job_b(NI, 1, 3)

            def job_c(h, par, c):
                buf = c % 2
                j = B * h + (JOBS_B + c)
                res = out_sb[par][:, c * CH:(c + 1) * CH]
                dve.wait_ge(dn_ready, B * h + (c + 1))
                nc.vector.scalar_tensor_tensor(res, ps[:, 2 * c + 1, :], bo_now[:, par:par + 1],
                                               xf_in[par][:, c * CH:(c + 1) * CH], ALU.add, ALU.add).then_inc(res_ok, 1)
                quantise(j, buf, sgn[:, buf, :])
                dve.wait_ge(q_ok, j + 1)
                dve.wait_ge(res_ok, B * h + (c + 1))
                nc.vector.tensor_tensor(res, res, sgn[:, buf, :], ALU.add).then_inc(out_ok, 1)

            def tile_c(h, par, loads, first=False, last=False):
                if not last:
                    dn_max(h + 1, 1 - par, 16 * h + 32)
                nc.vector.tensor_copy(bo_now[:, par:par + 1], bo[:, bass.ds(h, 1)]).then_inc(bo_ok, 1)
                dve.wait_ge(bo_ok, h + 1)
                if not last:
                    dn_scales(h + 1, 1 - par)
                    dn_errors(h + 1, 1 - par)
                dve.wait_ge(xf_in_ok[par], loads)
                if first is False:
                    dve.wait_ge(stored[par], store_count[0])
                for c in range(B):
                    job_c(h, par, c)

            store_count = [0]
            tile_c(0, 0, 16, first=True)
            tile_c(1, 1, 16, first=True)
            with dve.Fori(0, (HT - 2 - 2) // 2) as pair:
                h = pair * 2 + 2
                store_count[0] = h * (16 * B // 2)
                tile_c(h, 0, 8 * h + 16)
                tile_c(h + 1, 1, 8 * h + 16)
            store_count[0] = 16 * B * (HT // 2 - 1)
            tile_c(HT - 2, 0, 16 * HT // 2)
            tile_c(HT - 1, 1, 16 * HT // 2, last=True)

        @block.scalar
        def _(act):
            def std_devs(b):
                act.wait_ge(mv_ok, b + 1)
                nc.scalar.activation(std[:, :], mean_var[:, :, 1], ACT.Sqrt, bias=eps[:, 0:1]).then_inc(std_ok, 1)

            def x_high(b, tiles):
                for t in tiles:
                    act.wait_ge(xt_ready, b * TT + (t + 1))
                    src = ps[:, 2 * (t % 2):2 * (t % 2) + 2, :].rearrange("p a (k s) -> p (a k) s", s=P)
                    dst = xn[:, bass.ds(b, 1), :, :, t * P:(t + 1) * P].rearrange("p a l k s -> p (a l) k s")
                    nc.scalar.activation(dst[:, 0], src, ACT.Copy).then_inc(xhi_ok, 1)

            def high(w, scale, hi):
                nc.scalar.activation(hi, w, ACT.Copy, scale=scale).then_inc(whi_ok, 1)

            def low(done, err, scale, lo, total=None):
                act.wait_ge(werr_ok, done)
                nc.scalar.activation(lo, err, ACT.Copy, scale=scale).then_inc(wlo_ok, 1)
                if total is not None:
                    nc.scalar.activation(err, err, ACT.Abs, scale=scale, accum_out=total).then_inc(lo_sum_ok, 1)

            def flat(a):
                return a.rearrange("p k c -> p (k c)")

            def copy_qk(b):
                for f in range(2 * DT):
                    act.wait_ge(qk_ready, b * 4 + (f + 1))
                    dst = (q_t if f < DT else k_t)[:, f % DT, :]
                    nc.scalar.activation(dst, ps[:, f, :], ACT.Identity, bias=bqk[:, f:f + 1],
                                         scale=descale[:, 2 + f // DT, 0:1]).then_inc(qk_ok, 1)

            def exps(b):
                act.wait_ge(bias_ok, b + 1)
                for t in range(TT):
                    nc.scalar.activation(prob[:, t, :], ps[:, 4 + t, :], ACT.Exp, bias=soft_bias[:, t:t + 1],
                                         scale=SOFT, accum_out=row_sum[:, t:t + 1]).then_inc(exp_ok, 1)

            def copy_prob_t(b):
                for t in range(TT):
                    act.wait_ge(pt_ready, b * TT + (t + 1))
                    nc.scalar.activation(prob_t[:, :, t * P:(t + 1) * P],
                                         ps[:, 4 + t, :].rearrange("p (j s) -> p j s", s=P),
                                         ACT.Copy).then_inc(pt_ok, 1)

            def copy_attn(b):
                for d in range(DT):
                    act.wait_ge(pv_ready, b * DT + (d + 1))
                    nc.scalar.activation(attn_t[:, d, bass.ds(b * CH, CH)], ps[:, d, :], ACT.Copy).then_inc(attn_ok, 1)

            def gu_views(g, par, half, dst):
                if half:
                    return (gu_in[:, 0, g * GU // 2:(g + 1) * GU // 2].rearrange("p (k c) -> p k c", k=KT),
                            dst[:, 0, 0, :, g * HALF:(g + 1) * HALF])
                return gu_in[:, g, :], flat(dst[:, par, g, :, :])

            def gu_high(n, par, half=False):
                act.wait_ge(scales_ok, n + (QKV + 1))
                for g in range(2):
                    w, hi = gu_views(g, par, half, gu_hi)
                    high(w, to_unit[:, par, g:g + 1], hi)

            def gu_low(n, par, half=False):
                for g in range(2):
                    w, lo = gu_views(g, par, half, gu_lo)
                    low(2 * n + (2 * QKV + g + 1), w, to_unit_n[:, par, g:g + 1], lo, lo_sum[:, par, g:g + 1])

            def qkv_high(i):
                act.wait_ge(scales_ok, i + 1)
                for f in range(2 * i, 2 * i + 2):
                    high(wqkv_in[:, f * GU:(f + 1) * GU], to_unit[:, 2 + i, 0:1], flat(wqkv_hi[:, f, :, :]))

            def qkv_low(i):
                for f in range(2 * i, 2 * i + 2):
                    low(f + 1, wqkv_in[:, f * GU:(f + 1) * GU], to_unit_n[:, 2 + i, 0:1], flat(wqkv_lo[:, f, :, :]))

            act.wait_ge(eps_ok, 1)
            std_devs(0)
            x_high(0, range(0, 2))
            qkv_high(0)
            x_high(0, range(2, TT))
            for i in range(QKV):
                qkv_low(i)
                if i + 1 < QKV:
                    qkv_high(i + 1)
            std_devs(1)
            act.wait_ge(small_in, 48)
            copy_qk(0)

            def batch(b, more=True):
                x_high(b + 1, range(TT))
                exps(b)
                if more:
                    std_devs(b + 2)
                else:
                    gu_high(0, 0, half=True)
                    gu_low(0, 0, half=True)
                copy_qk(b + 1)
                copy_prob_t(b)
                copy_attn(b)

            with act.Fori(0, B - 2) as b:
                batch(b)
            batch(B - 2, more=False)
            exps(B - 1)

            def magnitude_sign(j, buf, n, src, scale, used, count):
                nonfirst = not (isinstance(j, int) and j < 2)
                if nonfirst:
                    act.wait_ge(rnd_ok, j - 1)
                nc.scalar.activation(mag[0:n, buf, :], src, ACT.Abs, scale=scale).then_inc(mag_ok, 1)
                if nonfirst:
                    act.wait_ge(used, count)
                nc.scalar.activation(sgn[0:n, buf, :], src, ACT.Sign, scale=scale).then_inc(sgn_ok, 1)

            def half_job(c):
                buf, j = c % 2, c
                bank = 2 + c % 2
                act.wait_ge(gu_ready, j + 1)
                nc.scalar.activation(sig[0:HALF, buf, :], ps[0:HALF, bank, :], ACT.Silu,
                                     scale=descale[0:HALF, 0, 0:1])
                if c >= 2:
                    act.wait_ge(rnd_ok, j - 1)
                nc.scalar.activation(mag[0:HALF, buf, :], ps[HALF:P, bank, :], ACT.Copy,
                                     scale=descale[HALF:P, 0, 1:2]).then_inc(silu_ok, 1)
                act.wait_ge(inter_ok, j + 1)
                magnitude_sign(j, buf, HALF, sig[0:HALF, buf, :], 1.0, q_ok, j - 1)

            half_job(0)
            gu_high(1, 1)
            half_job(1)
            copy_prob_t(B - 1)
            gu_low(1, 1)
            half_job(2)
            copy_attn(B - 1)
            half_job(3)

            def job_b(n, par, c):
                buf, j = c % 2, B * n + c
                act.wait_ge(gu_ready, j + 1)
                nc.scalar.activation(sig[:, buf, :], ps[:, 2 * c, :], ACT.Silu,
                                     scale=descale[:, par, 0:1]).then_inc(silu_ok, 1)
                act.wait_ge(inter_ok, j + 1)
                magnitude_sign(j, buf, P, sig[:, buf, :], 1.0, q_ok, j - 1)

            def tile_b(n, par):
                job_b(n, par, 0)
                gu_high(n + 1, 1 - par)
                gu_low(n + 1, 1 - par)
                for c in range(1, B):
                    job_b(n, par, c)

            with act.Fori(0, NI // 2) as pair:
                tile_b(pair * 2 + 1, 1)
                tile_b(pair * 2 + 2, 0)

            def dn_views(par, g, dst):
                n = DN // 2
                return (dn_in[:, g * n:(g + 1) * n], dst[par].rearrange("p i c -> p (i c)")[:, g * n:(g + 1) * n])

            def dn_high(h, par):
                act.wait_ge(scales_ok, h + (QKV + IT + 1))
                for g in range(2):
                    w, hi = dn_views(par, g, dn_hi)
                    high(w, to_unit[:, par, 0:1], hi)

            def dn_low(h, par):
                for g in range(2):
                    w, lo = dn_views(par, g, dn_lo)
                    low(2 * h + (2 * (QKV + IT) + g + 1), w, to_unit_n[:, par, 0:1], lo, lo_sum[:, par, g:g + 1])

            job_b(NI, 1, 0)
            job_b(NI, 1, 1)
            dn_high(0, 0)
            dn_low(0, 0)
            job_b(NI, 1, 2)
            job_b(NI, 1, 3)

            def job_c(h, par, c):
                buf = c % 2
                j = B * h + (JOBS_B + c)
                act.wait_ge(dn_ready, B * h + (c + 1))
                if isinstance(h, int) and B * h + c < 2:
                    used, count = q_ok, JOBS_B + c - 1
                else:
                    used, count = out_ok, B * h + (c - 1)
                magnitude_sign(j, buf, P, ps[:, 2 * c, :], descale[:, par, 0:1], used, count)

            def tile_c(h, par, last=False):
                if not last:
                    dn_high(h + 1, 1 - par)
                job_c(h, par, 0)
                if not last:
                    dn_low(h + 1, 1 - par)
                for c in range(1, B):
                    job_c(h, par, c)

            tile_c(0, 0)
            with act.Fori(0, (HT - 1 - 1) // 2) as pair:
                h = pair * 2 + 1
                tile_c(h, 1)
                tile_c(h + 1, 0)
            tile_c(HT - 1, 1, last=True)


def kernel(L0_attn_x, L0_attn_Wqkv, L0_attn_bqkv, L0_attn_Wo, L0_attn_bo, L0_ffn_w_gate, L0_ffn_w_up, L0_ffn_w_down):
    import concourse.bacc as bacc
    import numpy as np
    from concourse.bass_utils import run_bass_kernel_spmd

    batch, seq, hid = L0_attn_x.shape
    kt = hid // P
    nf = L0_attn_Wqkv.shape[1] // P
    inner = L0_ffn_w_gate.shape[0]
    ni, half = inner // P, P // 2
    x = np.asarray(L0_attn_x).reshape(batch * seq, hid)
    wqkv = np.asarray(L0_attn_Wqkv).reshape(kt, P, nf, P).transpose(1, 2, 0, 3).reshape(P, nf, kt * P)
    bqkv = np.asarray(L0_attn_bqkv)
    nqk = nf // 3 * 2

    def tiles(w, n):
        return w.reshape(-1, n, kt, P).transpose(0, 3, 2, 1)

    gate, up, down = (np.asarray(w) for w in (L0_ffn_w_gate, L0_ffn_w_up, L0_ffn_w_down))
    w_gu = np.stack([tiles(w[:ni * P], P).reshape(ni, P, kt * P) for w in (gate, up)], axis=2)
    w_gu_last = np.stack([tiles(w[ni * P:], half)[0].reshape(P, kt * half) for w in (gate, up)], axis=1)
    padded = np.zeros((hid, (ni + 1) * P), down.dtype)
    padded[:, :inner] = down
    w_down = padded.reshape(kt, P, ni + 1, P).transpose(0, 3, 2, 1).reshape(kt, P, (ni + 1) * P)
    wo = np.asarray(L0_attn_Wo).reshape(nf // 3, P, kt, P).transpose(2, 1, 0, 3)
    arrays = {
        "x_tok": x,
        "x_feat": x.T.reshape(kt, P, batch * seq),
        "w_qkv": wqkv,
        "b_qk": bqkv[:nqk * P].reshape(nqk, P).T,
        "b_v": bqkv[nqk * P:],
        "w_gu": w_gu,
        "w_gu_last": w_gu_last.reshape(P, kt * P),
        "w_down": w_down,
        "w_o": wo,
        "b_o": np.asarray(L0_attn_bo).reshape(kt, P).T,
    }
    arrays = {k: np.ascontiguousarray(a) for k, a in arrays.items()}
    nc = bacc.Bacc("TRN2", target_bir_lowering=False, num_devices=1)
    args = [nc.dram_tensor(k, a.shape, mybir.dt.from_np(a.dtype), kind="ExternalInput").ap() for k, a in arrays.items()]
    out = nc.dram_tensor("out", (kt, P, batch * seq), F32, kind="ExternalOutput").ap()
    build(nc, *args, out)
    r = run_bass_kernel_spmd(nc, [arrays], core_ids=[0])
    return r.results[0]["out"].reshape(hid, batch, seq).transpose(1, 2, 0)
```

```python
from contextlib import ExitStack

import concourse.bass as bass
from concourse import mybir

ALU = mybir.AluOpType
ACT = mybir.ActivationFunctionType
F32 = mybir.dt.float32
F16 = mybir.dt.float16
I32 = mybir.dt.int32
AX_X = mybir.AxisListType.X
ABSMAX = bass.bass_isa.ReduceOp.absmax

P = 128
W_UNIT = 8192.0
X_UNIT = 1024.0
HALVES = 2.0 ** 22
HALVES_UP = HALVES - 0.25
HALVES_DOWN = HALVES - 0.75
ONES = 2.0 ** 23
ONES_DOWN = 2.0 ** 23 + 1
TINY = 1e-30
EPS = 1e-5
VALUE_TOP = 2.0 ** 15
PROB_UNIT = 2.0 ** 14
ACT_Q = 128.0


def build(nc, x_tok, x_feat, w_qkv, b_qk, b_v, w_gu, w_gu_last, w_down, w_o, b_o, out):
    TOK, H = x_tok.shape
    KT = H // P
    CH = 512
    B = TOK // CH
    TT = CH // P
    NF = w_qkv.shape[1]
    QKV = 3
    DT = NF // QKV
    D = DT * P
    NI = w_gu.shape[0]
    HALF = P // 2
    IT = NI + 1
    HT = H // P
    SOFT = float(D) ** -0.5
    X_SUM = float(H)
    GU = KT * P
    DN = IT * P

    with ExitStack() as ctx:
        def sb(name, shape, dt):
            return ctx.enter_context(nc.sbuf_tensor(name, shape, dt))

        def sem(name):
            return ctx.enter_context(nc.semaphore(name))

        xn = sb("xn", [P, B, 2, KT, CH], F16)
        act_q = sb("act_q", [P, IT, TOK], F16)
        attn_t = sb("attn_t", [P, 2, DT, TOK], F16)
        gu_in = sb("gu_in", [P, 2, GU], F32)
        gu_hi = sb("gu_hi", [P, 2, 2, KT, P], F16)
        gu_lo = sb("gu_lo", [P, 2, 2, KT, P], F16)
        sig = sb("sig", [P, 2, CH], F32)
        mag = sb("mag", [P, 2, CH], F32)
        sgn = sb("sgn", [P, 2, CH], F16)
        rnd = sb("rnd", [P, CH], F32)
        tmp = sb("tmp", [P, CH], F32)
        ident = sb("ident", [P, P], F32)
        eps = sb("eps", [P, 1], F32)
        bqk = sb("bqk", [P, 2 * DT], F32)
        bo = sb("bo", [P, HT], F32)
        wmax = sb("wmax", [P, 2, 2], F32)
        gmax = sb("gmax", [P, 2, 2], F32)
        wtop = sb("wtop", [P, 2], F32)
        winv = sb("winv", [P, 2], F32)
        to_unit = sb("to_unit", [P, 2 + QKV, 2], F32)
        to_unit_n = sb("to_unit_n", [P, 2 + QKV, 2], F32)
        unit = sb("unit", [P, 2 + QKV, 2], F32)
        descale = sb("descale", [P, 2 + QKV, 2], F32)
        lo_sum = sb("lo_sum", [P, 2, 2], F32)
        lo_top = sb("lo_top", [P, 2], F32)
        has_lo = sb("has_lo", [P, 2], F32)
        stats = sb("stats", [P, TT, 2, 6], F32)
        mean_var = sb("mean_var", [P, TT, 2], F32)
        std = sb("std", [P, TT], F32)
        rstd = sb("rstd", [P, TT], F32)
        rstd_x = sb("rstd_x", [P, TT], F32)
        bias_col = sb("bias_col", [P, 2], F32)
        bias_max = sb("bias_max", [P, QKV], F32)
        bound = sb("bound", [P, QKV], F32)
        value_unit = sb("value_unit", [P, QKV], F32)
        per_value = sb("per_value", [P, QKV], F32)
        rescale = sb("rescale", [P, QKV], F32)
        score_unit = sb("score_unit", [P, 1], F32)
        soft_scale = sb("soft_scale", [P, 1], F32)
        neg_max = sb("neg_max", [P, TT], F32)
        soft_bias = sb("soft_bias", [P, TT], F32)
        row_sum = sb("row_sum", [P, TT], F32)
        row_inv = sb("row_inv", [P, TT], F32)
        fence = sb("fence", [P, 1], F32)
        first_max = sb("first_max", [P, 2], F32)
        bo_now = sb("bo_now", [P, 2], F32)

        neg_mean = rnd[:, 0:2]
        scratch = rnd[:, 2:3]

        a32 = act_q[:, :, :].rearrange("p a b -> p (a b)").bitcast(F32)
        place = [0]

        def in_a(n):
            place[0] += n
            assert place[0] <= IT * TOK // 2
            return a32[:, place[0] - n:place[0]]

        wqkv_in = in_a(NF * GU)
        wqkv_hi = in_a(NF * GU // 2).bitcast(F16).rearrange("p (f k c) -> p f k c", f=NF, k=KT)
        wqkv_lo = in_a(NF * GU // 2).bitcast(F16).rearrange("p (f k c) -> p f k c", f=NF, k=KT)
        x_in = in_a(TT * H).rearrange("p (t h) -> p t h", t=TT)
        qk_t = in_a(2 * DT * CH).rearrange("p (f s) -> p f s", f=2 * DT)
        v = in_a(TT * D).rearrange("p (t d) -> p t d", t=TT)
        v_parts = in_a(TT * D).bitcast(F16).rearrange("p (l t d) -> p l t d", l=2, t=TT)
        bv = in_a(D)
        assert place[0] <= NI * TOK // 2
        prob = wqkv_in[:, 0:TT * CH].rearrange("p (t s) -> p t s", t=TT)
        prob_t = wqkv_in[:, TT * CH:2 * TT * CH].bitcast(F16).rearrange("p (l t s) -> p l t s", l=2, t=TT)
        qk_parts = wqkv_in[:, 2 * TT * CH:2 * TT * CH + 2 * DT * CH].bitcast(F16).rearrange(
            "p (l f s) -> p l f s", l=2, f=2 * DT)

        def in_xn(b):
            return xn[:, b, :, :, :].rearrange("p a k s -> p (a k s)")

        dn_in = in_xn(0).bitcast(F32)[:, 0:DN]
        wo_in = in_xn(0).bitcast(F32)[:, DN:DN + DT * P]
        wo_parts = in_xn(0)[:, 2 * DN + 2 * DT * P:2 * DN + 6 * DT * P].rearrange(
            "p (b l n) -> p b l n", b=2, l=2)
        FIRST = 2 * GU // P
        first_pieces = [(gu_in[:, :, :].rearrange("p a n -> p (a n)"), 0, FIRST),
                        (dn_in[:, 0:DN - FIRST * P], FIRST, IT)]
        pieces = [(dn_in[:, 0:DN // 2], 0, IT // 2), (dn_in[:, DN // 2:DN], IT // 2, IT)]
        dn_hi = [in_xn(1 + i)[:, 0:DN].rearrange("p (i c) -> p i c", i=IT) for i in range(2)]
        dn_lo = [in_xn(1 + i)[:, DN:2 * DN].rearrange("p (i c) -> p i c", i=IT) for i in range(2)]
        xf_in = [in_xn(3).bitcast(F32)[:, i * TOK:(i + 1) * TOK] for i in range(2)]
        out_sb = [gu_hi[:, :, :, :, :].rearrange("p a b k c -> p (a b k c)").bitcast(F32)[:, 0:TOK],
                  gu_lo[:, :, :, :, :].rearrange("p a b k c -> p (a b k c)").bitcast(F32)[:, 0:TOK]]

        ps = ctx.enter_context(nc.psum_tensor("ps", [P, 8, CH], F32))

        ident0, ident_ok, eps_ok = sem("ident0"), sem("ident_ok"), sem("eps_ok")
        small_in = sem("small_in")
        wqkv_in_ok = [sem(f"wqkv_in_ok{i}") for i in range(QKV)]
        x_in_ok = [sem(f"x_in_ok{i}") for i in range(TT)]
        gu_in_ok, dn_in_ok, dn_first_ok = sem("gu_in_ok"), sem("dn_in_ok"), sem("dn_first_ok")
        wo_in_ok = sem("wo_in_ok")
        xf_in_ok = [sem(f"xf_in_ok{i}") for i in range(2)]
        stored = [sem(f"stored{i}") for i in range(2)]
        wmax_ok, gmax_ok, wtop_ok, winv_ok, scales_ok = (
            sem("wmax_ok"), sem("gmax_ok"), sem("wtop_ok"), sem("winv_ok"), sem("scales_ok"))
        whi_ok, werr_ok, wlo_ok = sem("whi_ok"), sem("werr_ok"), sem("wlo_ok")
        lo_sum_ok, lo_top_ok, has_lo_ok = sem("lo_sum_ok"), sem("lo_top_ok"), sem("has_lo_ok")
        stats_ok, mv_ok, std_ok, rstd_ok, rstd_x_ok, norm_ok = (
            sem("stats_ok"), sem("mv_ok"), sem("std_ok"), sem("rstd_ok"), sem("rstd_x_ok"), sem("norm_ok"))
        neg_mean_ok, norm_act_ok = sem("neg_mean_ok"), sem("norm_act_ok")
        xt_ready, xhi_ok, xlo_ok = sem("xt_ready"), sem("xhi_ok"), sem("xlo_ok")
        qk_ready, qk_ok, v_ready, v_ok = sem("qk_ready"), sem("qk_ok"), sem("v_ready"), sem("v_ok")
        s_ready, max_ok, bias_ok, exp_ok = sem("s_ready"), sem("max_ok"), sem("bias_ok"), sem("exp_ok")
        inv_ok, prob_ok, pt_ready, pt_ok = sem("inv_ok"), sem("prob_ok"), sem("pt_ready"), sem("pt_ok")
        pv_ready, attn_ok = sem("pv_ready"), sem("attn_ok")
        qk_lo_ok, v_hi_ok, v_lo_ok, pt_lo_ok, attn_lo_ok = (
            sem("qk_lo_ok"), sem("v_hi_ok"), sem("v_lo_ok"), sem("pt_lo_ok"), sem("attn_lo_ok"))
        bias_col_ok, bias_max_ok, bound_ok, value_unit_ok, per_value_ok, rescale_ok, soft_scale_ok = (
            sem("bias_col_ok"), sem("bias_max_ok"), sem("bound_ok"), sem("value_unit_ok"), sem("per_value_ok"),
            sem("rescale_ok"), sem("soft_scale_ok"))
        gu_ready, silu_ok, inter_ok, mag_ok, sgn_ok = (
            sem("gu_ready"), sem("silu_ok"), sem("inter_ok"), sem("mag_ok"), sem("sgn_ok"))
        rnd_ok, floor_ok, signed_ok, q_ok = sem("rnd_ok"), sem("floor_ok"), sem("signed_ok"), sem("q_ok")
        first_max_ok = sem("first_max_ok")
        dn_ready, res_ok, out_ok, bo_ok = sem("dn_ready"), sem("res_ok"), sem("out_ok"), sem("bo_ok")

        JOBS_B = IT * B

        block = ctx.enter_context(nc.Block())

        @block.sync
        def _(sp):
            def load_x(b):
                for t in range(TT):
                    sp.dma_start(x_in[:, t, :], x_tok[bass.ds(b * CH + t * P, P), :]).then_inc(x_in_ok[t], 16)

            load_x(0)
            for i in range(QKV):
                sp.dma_start(wqkv_in[:, 2 * i * GU:2 * (i + 1) * GU],
                             w_qkv[:, 2 * i:2 * i + 2, :].rearrange("p f n -> p (f n)")).then_inc(wqkv_in_ok[i], 16)
            sp.dma_start(bqk[:, :], b_qk).then_inc(small_in, 16)
            sp.dma_start(bo[:, :], b_o).then_inc(small_in, 16)
            sp.dma_start(bv, b_v.partition_broadcast(P)).then_inc(small_in, 16)
            sp.dma_start(gu_in[:, 0, :], w_gu_last).then_inc(gu_in_ok, 16)
            with sp.Fori(1, B) as b:
                sp.wait_ge(xt_ready, b * TT)
                load_x(b)
            with sp.Fori(1, IT) as n:
                sp.wait_ge(lo_sum_ok, 2 * n)
                sp.dma_start(gu_in[:, :, :], w_gu[bass.ds(n - 1, 1)].rearrange("a p g n -> p (a g) n")).then_inc(gu_in_ok, 16)
            sp.wait_ge(lo_sum_ok, 2 * IT)
            sp.dma_start(first_pieces[0][0], w_down[0][:, 0:FIRST * P]).then_inc(dn_first_ok, 16)
            sp.wait_ge(gu_ready, NI * B + 1)
            sp.dma_start(first_pieces[1][0], w_down[0][:, FIRST * P:DN]).then_inc(dn_in_ok, 16)
            sp.dma_start(wo_in, w_o[0].rearrange("p d c -> p (d c)")).then_inc(wo_in_ok, 16)
            sp.wait_ge(gu_ready, NI * B + B)
            sp.dma_start(xf_in[0], x_feat[0]).then_inc(xf_in_ok[0], 16)

            def load_down(h):
                sp.wait_ge(lo_sum_ok, 2 * h + 2 * IT)
                sp.dma_start(dn_in, w_down[bass.ds(h, 1)].rearrange("a p n -> p (a n)")).then_inc(dn_in_ok, 16)
                sp.dma_start(wo_in, w_o[bass.ds(h, 1)].rearrange("a p d c -> p (a d c)")).then_inc(wo_in_ok, 16)

            def load_x_feat(h, par):
                sp.dma_start(xf_in[par], x_feat[bass.ds(h, 1)].rearrange("a p n -> p (a n)")).then_inc(xf_in_ok[par], 16)

            def store(h, par, chunks):
                for c in chunks:
                    sp.wait_ge(out_ok, B * h + (c + 1))
                    sp.dma_start(out[bass.ds(h, 1)].rearrange("a p n -> p (a n)")[:, c * CH:(c + 1) * CH],
                                 out_sb[par][:, c * CH:(c + 1) * CH]).then_inc(stored[par], 16)

            def tile(h, par):
                store(h, par, [0])
                load_down(h + 2)
                store(h, par, range(1, B))
                load_x_feat(h + 2, par)

            load_down(1)
            load_x_feat(1, 1)
            tile(0, 0)
            with sp.Fori(0, (HT - 2) // 2 - 1) as pair:
                tile(pair * 2 + 1, 1)
                tile(pair * 2 + 2, 0)
            tile(HT - 3, 1)
            store(HT - 2, 0, range(B))
            store(HT - 1, 1, range(B))
            for par in range(2):
                sp.wait_ge(stored[par], 16 * B * HT // 2)

        @block.gpsimd
        def _(pool):
            nc.gpsimd.memset(ident[:, :], 0.0).then_inc(ident0, 1)
            nc.gpsimd.memset(eps[:, :], EPS).then_inc(eps_ok, 1)
            pool.wait_ge(ident0, 1)
            nc.gpsimd.affine_select(out=ident[:, :], in_=ident[:, :], compare_op=ALU.not_equal, fill=1.0,
                                    base=0, pattern=[[-1, P]], channel_multiplier=1).then_inc(ident_ok, 1)
            for blk in range(QKV + IT + HT):
                pool.wait_ge(wmax_ok, blk + 1)
                nc.gpsimd.partition_all_reduce(gmax[:, blk % 2, :], wmax[:, blk % 2, :], P, ABSMAX).then_inc(gmax_ok, 1)
                if blk == QKV - 1:
                    pool.wait_ge(bias_col_ok, 1)
                    nc.gpsimd.partition_all_reduce(bias_max[:, 0:2], bias_col[:, :], P, ABSMAX).then_inc(bias_max_ok, 1)
                if blk >= QKV:
                    n, par = blk - QKV, (blk - QKV) % 2
                    pool.wait_ge(lo_sum_ok, 2 * n + 2)
                    nc.gpsimd.partition_all_reduce(lo_top[:, :], lo_sum[:, par, :], P, ABSMAX).then_inc(lo_top_ok, 1)
                    pool.wait_ge(lo_top_ok, n + 1)
                    nc.gpsimd.tensor_tensor(has_lo[:, par:par + 1], lo_top[:, 0:1], lo_top[:, 1:2],
                                            ALU.add).then_inc(has_lo_ok, 1)

        @block.tensor
        def _(pe):
            def xpart(b, part, k, lo, n):
                if isinstance(b, int):
                    return xn[:, b, part, k, lo:lo + n]
                return xn[:, bass.ds(b, 1), part, k, lo:lo + n].rearrange("p a s -> p (a s)")

            def transposes(b, tiles, first=False):
                for t in tiles:
                    pe.wait_ge(norm_ok, b * TT + (t + 1))
                    if first and t >= 2:
                        pe.wait_ge(norm_act_ok, t - 1)
                    if t >= 2:
                        pe.wait_ge(xhi_ok, b * TT + (t - 1))
                        pe.wait_ge(xlo_ok, b * TT + (t - 1))
                    for k in range(KT):
                        mm = nc.tensor.transpose(ps[:, 2 * (t % 2) + k // 4, (k % 4) * P:(k % 4 + 1) * P],
                                                 x_in[:, t, k * P:(k + 1) * P], ident[:, :])
                    mm.then_inc(xt_ready, 1)

            def first_queries_keys():
                for f in range(2 * DT):
                    if f == 0:
                        pe.wait_ge(xhi_ok, TT)
                    pe.wait_ge(whi_ok, f + 1)
                    for k in range(KT):
                        nc.tensor.matmul(ps[:, 4 + f, :], wqkv_hi[:, f, k, :], xpart(0, 0, k, 0, CH),
                                         start=(k == 0), stop=False)
                    pe.wait_ge(wlo_ok, f + 1)
                    for k in range(KT):
                        nc.tensor.matmul(ps[:, 4 + f, :], wqkv_lo[:, f, k, :], xpart(0, 0, k, 0, CH),
                                         start=False, stop=False)
                    if f == 0:
                        pe.wait_ge(xlo_ok, TT)
                    for k in range(KT):
                        mm = nc.tensor.matmul(ps[:, 4 + f, :], wqkv_hi[:, f, k, :], xpart(0, 1, k, 0, CH),
                                              start=False, stop=(k == KT - 1))
                    mm.then_inc(qk_ready, 1)

            def queries_keys(b):
                pe.wait_ge(xhi_ok, b * TT + TT)
                pe.wait_ge(xlo_ok, b * TT + TT)
                for f in range(2 * DT):
                    for k in range(KT):
                        nc.tensor.matmul(ps[:, f, :], wqkv_hi[:, f, k, :], xpart(b, 0, k, 0, CH),
                                         start=(k == 0), stop=False)
                        nc.tensor.matmul(ps[:, f, :], wqkv_hi[:, f, k, :], xpart(b, 1, k, 0, CH),
                                         start=False, stop=False)
                        mm = nc.tensor.matmul(ps[:, f, :], wqkv_lo[:, f, k, :], xpart(b, 0, k, 0, CH),
                                              start=False, stop=(k == KT - 1))
                    mm.then_inc(qk_ready, 1)

            def values(b):
                for t in range(TT):
                    dst = ps[:, 2 + t // 2, (t % 2) * D:(t % 2 + 1) * D]
                    for k in range(KT):
                        nc.tensor.matmul(dst, xpart(b, 0, k, t * P, P), wqkv_hi[:, 2 * DT:NF, k, :],
                                         start=(k == 0), stop=False)
                        nc.tensor.matmul(dst, xpart(b, 0, k, t * P, P), wqkv_lo[:, 2 * DT:NF, k, :],
                                         start=False, stop=False)
                        mm = nc.tensor.matmul(dst, xpart(b, 1, k, t * P, P), wqkv_hi[:, 2 * DT:NF, k, :],
                                              start=False, stop=(k == KT - 1))
                    if t % 2:
                        mm.then_inc(v_ready, 1)

            def scores(b, tiles):
                for t in tiles:
                    for d in range(DT):
                        for i, (q_lo, k_lo) in enumerate(((0, 0), (0, 1), (1, 0))):
                            mm = nc.tensor.matmul(ps[:, 4 + t, :], qk_parts[:, q_lo, d, t * P:(t + 1) * P],
                                                  qk_parts[:, k_lo, DT + d, :],
                                                  start=(d == 0 and i == 0), stop=(d == DT - 1 and i == 2))
                    mm.then_inc(s_ready, 1)

            def transpose_probs(b):
                for t in range(TT):
                    pe.wait_ge(prob_ok, b * TT + (t + 1))
                    for j in range(TT):
                        mm = nc.tensor.transpose(ps[:, 4 + t, j * P:(j + 1) * P],
                                                 prob[:, t, j * P:(j + 1) * P], ident[:, :])
                    mm.then_inc(pt_ready, 1)

            def attend(b):
                pe.wait_ge(v_lo_ok, b + 1)
                pe.wait_ge(pt_lo_ok, b * TT + TT)
                for d in range(DT):
                    for j in range(TT):
                        for i, (v_lo, p_lo) in enumerate(((0, 0), (0, 1), (1, 0))):
                            mm = nc.tensor.matmul(ps[:, 6 + d, :], v_parts[:, v_lo, j, d * P:(d + 1) * P],
                                                  prob_t[:, p_lo, j, :],
                                                  start=(j == 0 and i == 0), stop=(j == TT - 1 and i == 2))
                    mm.then_inc(pv_ready, 1)

            low_reg = pe.alloc_register("low_parts")

            def batch(b):
                transposes(b + 1, [0])
                pe.wait_ge(v_ok, b * TT + TT)
                transposes(b + 1, [1])
                pe.wait_ge(qk_lo_ok, b * 4 + 4)
                scores(b, range(0, 2))
                transposes(b + 1, range(2, TT))
                pe.wait_ge(v_lo_ok, b + 1)
                scores(b, range(2, TT))
                queries_keys(b + 1)
                transpose_probs(b)
                pe.wait_ge(qk_ok, b * 4 + 8)
                values(b + 1)
                attend(b)

            pe.wait_ge(ident_ok, 1)
            transposes(0, range(TT), first=True)
            first_queries_keys()
            pe.wait_ge(wlo_ok, 2 * QKV)
            values(0)
            with pe.Fori(0, B - 2) as b:
                batch(b)
            batch(B - 2)
            pe.wait_ge(qk_lo_ok, B * 4)
            scores(B - 1, range(0, 2))
            pe.wait_ge(v_lo_ok, B)
            scores(B - 1, range(2, TT))

            def parts_made(n):
                pe.wait_ge(wlo_ok, 2 * n + (2 * QKV + 2))
                pe.wait_ge(has_lo_ok, n + 1)

            def down_parts_made(h):
                pe.wait_ge(wlo_ok, 3 * h + (2 * (QKV + IT) + 3))
                pe.wait_ge(has_lo_ok, h + (IT + 1))

            def by_low_parts(par, body):
                pe.reg_load(low_reg, has_lo[0:1, par:par + 1].bitcast(I32))
                with pe.If_ne(low_reg, 0):
                    body(True)
                with pe.Else():
                    body(False)

            def gate_up_job(dst, par, g, c, low, following=None):
                for k in range(KT):
                    nc.tensor.matmul(dst, gu_hi[:, par, g, k, :], xn[:, c, 0, k, :], start=(k == 0), stop=False)
                    if low:
                        nc.tensor.matmul(dst, gu_lo[:, par, g, k, :], xn[:, c, 0, k, :], start=False, stop=False)
                    if k == KT - 1 and following is not None:
                        parts_made(following)
                    mm = nc.tensor.matmul(dst, gu_hi[:, par, g, k, :], xn[:, c, 1, k, :],
                                          start=False, stop=(k == KT - 1))
                return mm

            def half_block(low):
                for c in range(B):
                    if c >= 2:
                        pe.wait_ge(inter_ok, c - 1)
                    gate_up_job(ps[:, 2 + c % 2, :], 0, 0, c, low, 1 if c == B - 1 else None).then_inc(gu_ready, 1)
                    if c == 1:
                        transpose_probs(B - 1)
                    if c == 2:
                        attend(B - 1)

            parts_made(0)
            by_low_parts(0, half_block)

            def gate_up(n, par, first=False, following=True):
                def jobs(low):
                    for c in range(B):
                        if not first:
                            pe.wait_ge(inter_ok, B * n + (c + 1 - B))
                        elif c == 3:
                            pe.wait_ge(attn_lo_ok, B * DT)
                        elif c == 1:
                            pe.wait_ge(inter_ok, B)
                        gate_up_job(ps[:, 2 * c, :], par, 0, c, low)
                        gate_up_job(ps[:, 2 * c + 1, :], par, 1, c, low,
                                    n + 1 if c == B - 1 and following else None).then_inc(gu_ready, 1)

                by_low_parts(par, jobs)

            gate_up(1, 1, first=True)
            with pe.Fori(1, NI // 2) as pair:
                gate_up(pair * 2, 0)
                gate_up(pair * 2 + 1, 1)
            gate_up(NI - 1, 0)
            gate_up(NI, 1, following=False)

            def project(c, par, following=None):
                for d in range(DT):
                    for i, (w_lo, a_lo) in enumerate(((0, 0), (0, 1), (1, 0))):
                        if d == DT - 1 and i == 2 and following is not None:
                            down_parts_made(following)
                        mm = nc.tensor.matmul(ps[:, 2 * c + 1, :], wo_parts[:, par, w_lo, d * P:(d + 1) * P],
                                              attn_t[:, a_lo, d, c * CH:(c + 1) * CH],
                                              start=(d == 0 and i == 0), stop=(d == DT - 1 and i == 2))
                return mm

            def down(h, par, first=False, last=False):
                def jobs(low):
                    for c in range(B):
                        dst = ps[:, 2 * c, :]
                        if first:
                            pe.wait_ge(q_ok, B * NI + (c + 1))
                        else:
                            pe.wait_ge(res_ok, B * h + (c + 1 - B))
                            pe.wait_ge(sgn_ok, B * h + (JOBS_B + c + 1 - B))
                        for i in range(IT):
                            n = P if i < NI else HALF
                            q = act_q[0:n, i, c * CH:(c + 1) * CH]
                            if low:
                                nc.tensor.matmul(dst, dn_lo[par][0:n, i, :], q, start=(i == 0), stop=False)
                            if first and c == B - 1 and i == IT - 1:
                                down_parts_made(h + 1)
                            mm = nc.tensor.matmul(dst, dn_hi[par][0:n, i, :], q,
                                                  start=(i == 0 and not low), stop=(i == IT - 1))
                        if not first:
                            mm = project(c, par, h + 1 if c == B - 1 and not last else None)
                        mm.then_inc(dn_ready, 1)

                by_low_parts(par, jobs)

            pe.wait_ge(wlo_ok, 2 * (QKV + IT) + 1)
            for c in range(B):
                pe.wait_ge(inter_ok, B * NI + (c + 1))
                project(c, 0)
            down_parts_made(0)
            down(0, 0, first=True)
            with pe.Fori(0, (HT - 2) // 2) as pair:
                h = pair * 2 + 1
                down(h, 1)
                down(h + 1, 0)
            down(HT - 1, 1, last=True)

        @block.vector
        def _(dve):
            def block_max(blk, par, src, loaded, count):
                dve.wait_ge(loaded, count)
                nc.vector.tensor_reduce(wmax[:, par, :], src, AX_X, ALU.max, apply_absolute_value=True).then_inc(wmax_ok, 1)

            def block_scales(blk, par, place, one, to_value0, to_value1, per=None):
                dve.wait_ge(gmax_ok, blk + 1)
                if one:
                    nc.vector.scalar_tensor_tensor(wtop[:, 0:1], gmax[:, par, 0:1], TINY, gmax[:, par, 1:2],
                                                   ALU.max, ALU.max)
                    nc.vector.scalar_tensor_tensor(wtop[:, 1:2], gmax[:, par, 0:1], TINY, gmax[:, par, 1:2],
                                                   ALU.max, ALU.max).then_inc(wtop_ok, 1)
                else:
                    nc.vector.tensor_scalar(wtop[:, :], gmax[:, par, :], TINY, None, ALU.max).then_inc(wtop_ok, 1)
                dve.wait_ge(wtop_ok, blk + 1)
                nc.vector.reciprocal(winv[:, :], wtop[:, :]).then_inc(winv_ok, 1)
                nc.vector.tensor_scalar(unit[:, place, :], wtop[:, :], 1.0 / W_UNIT, None, ALU.mult)
                nc.vector.tensor_scalar(descale[:, place, 0:1], wtop[:, 0:1], to_value0, None, ALU.mult)
                if per is None:
                    nc.vector.tensor_scalar(descale[:, place, 1:2], wtop[:, 1:2], to_value1, None, ALU.mult)
                else:
                    nc.vector.tensor_scalar(descale[:, place, 1:2], wtop[:, 1:2], per, to_value1, ALU.mult, ALU.mult)
                dve.wait_ge(winv_ok, blk + 1)
                nc.vector.tensor_scalar(to_unit[:, place, :], winv[:, :], W_UNIT, None, ALU.mult)
                nc.vector.tensor_scalar(to_unit_n[:, place, :], winv[:, :], -W_UNIT, None, ALU.mult).then_inc(scales_ok, 1)

            def part_error(done, hi, scale, w):
                dve.wait_ge(whi_ok, done)
                nc.vector.scalar_tensor_tensor(w, hi, scale, w, ALU.mult, ALU.subtract).then_inc(werr_ok, 1)

            QKV_VALUE = 1.0 / (W_UNIT * X_UNIT)
            GU_VALUE = QKV_VALUE / ACT_Q
            DN_VALUE = ACT_Q / W_UNIT

            def qkv_max(i):
                block_max(i, i % 2, wqkv_in[:, 2 * i * GU:2 * (i + 1) * GU].rearrange("p (g n) -> p g n", g=2),
                          wqkv_in_ok[i], 16)

            def qkv_scales(i):
                block_scales(i, i % 2, 2 + i, True, QKV_VALUE, QKV_VALUE)

            def qkv_errors(i):
                for f in range(2 * i, 2 * i + 2):
                    part_error(f + 1, wqkv_hi[:, f, :, :].rearrange("p k c -> p (k c)"), unit[:, 2 + i, 0:1],
                               wqkv_in[:, f * GU:(f + 1) * GU])

            def gu_max(n, par, half=False):
                src = gu_in[:, 0, :].rearrange("p (g n) -> p g n", g=2) if half else gu_in[:, :, :]
                block_max(n + QKV, 1 - par, src, gu_in_ok, 16 * n + 16)

            def gu_scales(n, par):
                block_scales(n + QKV, 1 - par, par, False, GU_VALUE, GU_VALUE * ACT_Q)

            def gu_errors(n, par, half=False):
                for g in range(2):
                    if half:
                        hi = gu_hi[:, 0, 0, :, g * HALF:(g + 1) * HALF]
                        w = gu_in[:, 0, g * GU // 2:(g + 1) * GU // 2].rearrange("p (k c) -> p k c", k=KT)
                    else:
                        hi = gu_hi[:, par, g, :, :].rearrange("p k c -> p (k c)")
                        w = gu_in[:, g, :]
                    part_error(2 * n + (2 * QKV + g + 1), hi, unit[:, par, g:g + 1], w)

            def normalise(b, first=False):
                for t in range(TT):
                    dve.wait_ge(x_in_ok[t], 16 * b + 16)
                    for i in range(2):
                        st = nc.vector.bn_stats(stats[:, t, i, :], x_in[:, t, i * CH:(i + 1) * CH])
                    st.then_inc(stats_ok, 1)
                dve.wait_ge(stats_ok, b * TT + TT)
                nc.vector.memset(fence[:, :], 0.0)
                for t in range(TT):
                    ag = nc.vector.bn_aggr(mean_var[:, t, :], stats[:, t, :, :].rearrange("p i s -> p (i s)"))
                ag.then_inc(mv_ok, 1)
                dve.wait_ge(std_ok, b + 1)
                nc.vector.reciprocal(rstd[:, :], std[:, :]).then_inc(rstd_ok, 1)
                dve.wait_ge(rstd_ok, b + 1)
                nc.vector.tensor_scalar(rstd_x[:, :], rstd[:, :], X_UNIT, None, ALU.mult).then_inc(rstd_x_ok, 1)
                dve.wait_ge(rstd_x_ok, b + 1)
                if first:
                    nc.vector.scalar_tensor_tensor(neg_mean[:, :], mean_var[:, 2:TT, 0], -1.0, rstd_x[:, 2:TT],
                                                   ALU.mult, ALU.mult).then_inc(neg_mean_ok, 1)
                for t in range(2 if first else TT):
                    nc.vector.tensor_scalar(x_in[:, t, :], x_in[:, t, :], mean_var[:, t, 0:1], rstd_x[:, t:t + 1],
                                            ALU.subtract, ALU.mult).then_inc(norm_ok, 3 if first and t == 1 else 1)

            def x_low(b, tiles):
                for t in tiles:
                    dve.wait_ge(xhi_ok, b * TT + (t + 1))
                    src = ps[:, 2 * (t % 2):2 * (t % 2) + 2, :].rearrange("p a (k s) -> p (a k) s", s=P)
                    dst = xn[:, bass.ds(b, 1), :, :, t * P:(t + 1) * P].rearrange("p a l k s -> p (a l) k s")
                    nc.vector.tensor_tensor(dst[:, 1], src, dst[:, 0], ALU.subtract).then_inc(xlo_ok, 1)

            def row_maxima(b, tiles):
                for t in tiles:
                    dve.wait_ge(s_ready, b * TT + (t + 1))
                    nc.vector.tensor_reduce(neg_max[:, t:t + 1], ps[:, 4 + t, :], AX_X, ALU.max,
                                            negate=True).then_inc(max_ok, 1)

            def exponent_biases(b):
                dve.wait_ge(max_ok, b * TT + TT)
                nc.vector.tensor_scalar(soft_bias[:, :], neg_max[:, :], soft_scale[:, 0:1], None, ALU.mult).then_inc(bias_ok, 1)

            def soft_normalise(b):
                dve.wait_ge(exp_ok, b * TT + TT)
                nc.vector.reciprocal(row_inv[:, :], row_sum[:, :]).then_inc(inv_ok, 1)
                dve.wait_ge(inv_ok, b + 1)
                for t in range(TT):
                    nc.vector.tensor_scalar(prob[:, t, :], prob[:, t, :], row_inv[:, t:t + 1], PROB_UNIT,
                                            ALU.mult, ALU.mult).then_inc(prob_ok, 1)

            def copy_v(b):
                for t in range(TT):
                    if t % 2 == 0:
                        dve.wait_ge(v_ready, b * (TT // 2) + (t // 2 + 1))
                    nc.vector.scalar_tensor_tensor(v[:, t, :], ps[:, 2 + t // 2, (t % 2) * D:(t % 2 + 1) * D],
                                                   rescale[:, 2:3], bv, ALU.mult, ALU.add).then_inc(v_ok, 1)

            def v_low(b):
                dve.wait_ge(v_hi_ok, b + 1)
                nc.vector.tensor_tensor(v_parts[:, 1, :, :], v[:, :, :], v_parts[:, 0, :, :],
                                        ALU.subtract).then_inc(v_lo_ok, 1)

            def qk_low(b):
                for f in range(2 * DT):
                    dve.wait_ge(qk_ok, b * 4 + (f + 1))
                    nc.vector.tensor_tensor(qk_parts[:, 1, f, :], qk_t[:, f, :], qk_parts[:, 0, f, :],
                                            ALU.subtract).then_inc(qk_lo_ok, 1)

            def prob_t_low(b):
                for t in range(TT):
                    dve.wait_ge(pt_ok, b * TT + (t + 1))
                    cols = slice(t * P, (t + 1) * P)
                    nc.vector.tensor_tensor(prob_t[:, 1, :, cols], ps[:, 4 + t, :].rearrange("p (j s) -> p j s", s=P),
                                            prob_t[:, 0, :, cols], ALU.subtract).then_inc(pt_lo_ok, 1)

            def attn_low(b):
                for d in range(DT):
                    dve.wait_ge(attn_ok, b * DT + (d + 1))
                    toks = bass.ds(b * CH, CH)
                    nc.vector.scalar_tensor_tensor(attn_t[:, 1, d, toks], ps[:, 6 + d, :], 1.0 / PROB_UNIT,
                                                   attn_t[:, 0, d, toks], ALU.mult, ALU.subtract).then_inc(attn_lo_ok, 1)

            def bias_maxima():
                dve.wait_ge(small_in, 48)
                nc.vector.tensor_reduce(bias_col[:, :], bqk[:, :].rearrange("p (i d) -> p i d", i=2), AX_X, ALU.max,
                                        apply_absolute_value=True).then_inc(bias_col_ok, 1)
                nc.vector.tensor_reduce(bias_max[:, 2:3], bv, AX_X, ALU.max,
                                        apply_absolute_value=True).then_inc(bias_max_ok, 1)

            def value_scales():
                dve.wait_ge(bias_max_ok, 2)
                dve.wait_ge(scales_ok, QKV)
                nc.vector.scalar_tensor_tensor(bound[:, :], unit[:, 2:2 + QKV, 0], W_UNIT * X_SUM, bias_max[:, :],
                                               ALU.mult, ALU.add).then_inc(bound_ok, 1)
                dve.wait_ge(bound_ok, 1)
                nc.vector.tensor_scalar(value_unit[:, :], bound[:, :], 1.0 / VALUE_TOP, None,
                                        ALU.mult).then_inc(value_unit_ok, 1)
                dve.wait_ge(value_unit_ok, 1)
                nc.vector.reciprocal(per_value[:, :], value_unit[:, :]).then_inc(per_value_ok, 1)
                nc.vector.tensor_tensor(score_unit[:, :], value_unit[:, 0:1], value_unit[:, 1:2],
                                        ALU.mult).then_inc(value_unit_ok, 1)
                dve.wait_ge(value_unit_ok, 2)
                nc.vector.tensor_scalar(soft_scale[:, :], score_unit[:, :], SOFT, None, ALU.mult).then_inc(soft_scale_ok, 1)
                dve.wait_ge(per_value_ok, 1)
                nc.vector.tensor_tensor(rescale[:, :], descale[:, 2:2 + QKV, 0], per_value[:, :], ALU.mult)
                for i in range(2):
                    nc.vector.tensor_scalar(bqk[:, i * DT:(i + 1) * DT], bqk[:, i * DT:(i + 1) * DT],
                                            per_value[:, i:i + 1], None, ALU.mult)
                nc.vector.tensor_scalar(bv, bv, per_value[:, 2:3], None, ALU.mult).then_inc(rescale_ok, 1)

            normalise(0, first=True)
            qkv_max(0)
            x_low(0, range(0, 2))
            qkv_scales(0)
            qkv_max(1)
            qkv_errors(0)
            x_low(0, range(2, TT))
            qkv_scales(1)
            qkv_errors(1)
            qkv_max(2)
            bias_maxima()
            qkv_scales(2)
            qkv_errors(2)
            value_scales()
            normalise(1)
            qk_low(0)
            dve.wait_ge(rescale_ok, 1)
            copy_v(0)
            v_low(0)

            def batch(b, more=True):
                x_low(b + 1, range(0, 2))
                row_maxima(b, range(0, 2))
                x_low(b + 1, range(2, TT))
                row_maxima(b, range(2, TT))
                exponent_biases(b)
                soft_normalise(b)
                if more:
                    normalise(b + 2)
                else:
                    gu_max(0, 0, half=True)
                    gu_scales(0, 0)
                    gu_errors(0, 0, half=True)
                qk_low(b + 1)
                prob_t_low(b)

            with dve.Fori(0, B - 2) as b:
                batch(b)
                copy_v(b + 1)
                attn_low(b)
                v_low(b + 1)
            batch(B - 2, more=False)
            copy_v(B - 1)
            attn_low(B - 2)
            v_low(B - 1)
            row_maxima(B - 1, range(TT))
            exponent_biases(B - 1)
            gu_max(1, 1)
            soft_normalise(B - 1)
            gu_scales(1, 1)

            def quantise(j, buf, dst):
                n = dst.shape[0]
                dve.wait_ge(mag_ok, j + 1)
                nc.vector.tensor_scalar(rnd[0:n], mag[0:n, buf, :], HALVES_UP, HALVES,
                                        ALU.add, ALU.max).then_inc(rnd_ok, 1)
                dve.wait_ge(rnd_ok, j + 1)
                nc.vector.tensor_scalar(tmp[0:n], rnd[0:n], HALVES_DOWN, ONES,
                                        ALU.subtract, ALU.add).then_inc(floor_ok, 1)
                dve.wait_ge(floor_ok, j + 1)
                dve.wait_ge(sgn_ok, j + 1)
                nc.vector.scalar_tensor_tensor(sgn[0:n, buf, :], tmp[0:n], ONES_DOWN, sgn[0:n, buf, :],
                                               ALU.subtract, ALU.mult).then_inc(signed_ok, 1)
                dve.wait_ge(signed_ok, j + 1)
                nc.vector.tensor_scalar(dst, sgn[0:n, buf, :], 127.0, -128.0, ALU.min, ALU.max).then_inc(q_ok, 1)

            def job_b(n, par, c):
                buf = c % 2
                j = B * n + c
                dve.wait_ge(silu_ok, j + 1)
                nc.vector.scalar_tensor_tensor(sig[:, buf, :], ps[:, 2 * c + 1, :], descale[:, par, 1:2],
                                               sig[:, buf, :], ALU.mult, ALU.mult).then_inc(inter_ok, 1)
                quantise(j, buf, act_q[:, bass.ds(n - 1, 1), c * CH:(c + 1) * CH].rearrange("p a s -> p (a s)"))

            for c in range(B):
                buf, j = c % 2, c
                dve.wait_ge(silu_ok, j + 1)
                nc.vector.tensor_tensor(sig[0:HALF, buf, :], sig[0:HALF, buf, :], mag[0:HALF, buf, :],
                                        ALU.mult).then_inc(inter_ok, 1)
                quantise(j, buf, act_q[0:HALF, NI, c * CH:(c + 1) * CH])
                if c == 0:
                    prob_t_low(B - 1)
                    gu_errors(1, 1)
                if c == 2:
                    attn_low(B - 1)
            dve.wait_ge(attn_lo_ok, B * DT)

            def tile_b(n, par):
                gu_max(n + 1, 1 - par)
                job_b(n, par, 0)
                gu_scales(n + 1, 1 - par)
                gu_errors(n + 1, 1 - par)
                for c in range(1, B):
                    job_b(n, par, c)

            with dve.Fori(0, NI // 2) as pair:
                tile_b(pair * 2 + 1, 1)
                tile_b(pair * 2 + 2, 0)

            def first_piece_max(i, loaded):
                dve.wait_ge(loaded, 16)
                nc.vector.tensor_reduce(first_max[:, i:i + 1], first_pieces[i][0], AX_X, ALU.max,
                                        apply_absolute_value=True).then_inc(first_max_ok, 1)

            def dn_max(h, par, count, first=False):
                if first:
                    first_piece_max(1, dn_in_ok)
                    dve.wait_ge(first_max_ok, 2)
                    nc.vector.tensor_reduce(wmax[:, 1 - par, 0:1], first_max[:, :], AX_X, ALU.max)
                else:
                    dve.wait_ge(dn_in_ok, count)
                    nc.vector.tensor_reduce(wmax[:, 1 - par, 0:1], dn_in, AX_X, ALU.max, apply_absolute_value=True)
                dve.wait_ge(wo_in_ok, count)
                nc.vector.tensor_reduce(wmax[:, 1 - par, 1:2], wo_in, AX_X, ALU.max,
                                        apply_absolute_value=True).then_inc(wmax_ok, 1)

            def dn_scales(h, par):
                block_scales(h + (QKV + IT), 1 - par, par, False, DN_VALUE, 1.0 / W_UNIT, value_unit[:, 2:3])

            def dn_errors(h, par, places=pieces):
                part_error(3 * h + (2 * (QKV + IT) + 1), wo_parts[:, par, 0, :], unit[:, par, 1:2], wo_in)
                for g, (w, lo, hi) in enumerate(places):
                    part_error(3 * h + (2 * (QKV + IT) + g + 2), dn_hi[par][:, lo:hi, :].rearrange("p i c -> p (i c)"),
                               unit[:, par, 0:1], w)

            first_piece_max(0, dn_first_ok)
            job_b(NI, 1, 0)
            dn_max(0, 0, 16, first=True)
            dn_scales(0, 0)
            job_b(NI, 1, 1)
            dn_errors(0, 0, first_pieces)
            job_b(NI, 1, 2)
            job_b(NI, 1, 3)
            dn_max(1, 1, 32)

            def job_c(h, par, c):
                buf = c % 2
                j = B * h + (JOBS_B + c)
                res = out_sb[par][:, c * CH:(c + 1) * CH]
                dve.wait_ge(dn_ready, B * h + (c + 1))
                nc.vector.scalar_tensor_tensor(res, ps[:, 2 * c + 1, :], descale[:, par, 1:2],
                                               xf_in[par][:, c * CH:(c + 1) * CH], ALU.mult, ALU.add).then_inc(res_ok, 1)
                quantise(j, buf, sgn[:, buf, :])
                dve.wait_ge(q_ok, j + 1)
                dve.wait_ge(res_ok, B * h + (c + 1))
                nc.vector.scalar_tensor_tensor(res, sgn[:, buf, :], bo_now[:, par:par + 1], res,
                                               ALU.add, ALU.add).then_inc(out_ok, 1)

            def tile_c(h, par, loads, first=False, last=0):
                nc.vector.tensor_copy(bo_now[:, par:par + 1], bo[:, bass.ds(h, 1)]).then_inc(bo_ok, 1)
                dve.wait_ge(bo_ok, h + 1)
                if last < 2:
                    dn_scales(h + 1, 1 - par)
                    dn_errors(h + 1, 1 - par)
                dve.wait_ge(xf_in_ok[par], loads)
                if first is False:
                    dve.wait_ge(stored[par], store_count[0])
                for c in range(B):
                    if c == B - 1 and last == 0:
                        dn_max(h + 2, par, 16 * h + 48)
                    job_c(h, par, c)

            store_count = [0]
            tile_c(0, 0, 16, first=True)
            tile_c(1, 1, 16, first=True)
            with dve.Fori(0, (HT - 2 - 2) // 2) as pair:
                h = pair * 2 + 2
                store_count[0] = h * (16 * B // 2)
                tile_c(h, 0, 8 * h + 16)
                tile_c(h + 1, 1, 8 * h + 16)
            store_count[0] = 16 * B * (HT // 2 - 1)
            tile_c(HT - 2, 0, 16 * HT // 2, last=1)
            tile_c(HT - 1, 1, 16 * HT // 2, last=2)

        @block.scalar
        def _(act):
            def std_devs(b):
                act.wait_ge(mv_ok, b + 1)
                nc.scalar.activation(std[:, :], mean_var[:, :, 1], ACT.Sqrt, bias=eps[:, 0:1]).then_inc(std_ok, 1)

            def x_high(b, tiles):
                for t in tiles:
                    act.wait_ge(xt_ready, b * TT + (t + 1))
                    src = ps[:, 2 * (t % 2):2 * (t % 2) + 2, :].rearrange("p a (k s) -> p (a k) s", s=P)
                    dst = xn[:, bass.ds(b, 1), :, :, t * P:(t + 1) * P].rearrange("p a l k s -> p (a l) k s")
                    nc.scalar.activation(dst[:, 0], src, ACT.Copy).then_inc(xhi_ok, 1)

            def high(w, scale, hi):
                nc.scalar.activation(hi, w, ACT.Copy, scale=scale).then_inc(whi_ok, 1)

            def low(done, err, scale, lo, total=None):
                act.wait_ge(werr_ok, done)
                nc.scalar.activation(lo, err, ACT.Copy, scale=scale).then_inc(wlo_ok, 1)
                if total is not None:
                    nc.scalar.activation(err, err, ACT.Abs, scale=scale, accum_out=total).then_inc(lo_sum_ok, 1)

            def flat(a):
                return a.rearrange("p k c -> p (k c)")

            def copy_qk(b, bank=0):
                for f in range(2 * DT):
                    act.wait_ge(qk_ready, b * 4 + (f + 1))
                    i = f // DT
                    nc.scalar.activation(qk_t[:, f, :], ps[:, bank + f, :], ACT.Identity, bias=bqk[:, f:f + 1],
                                         scale=rescale[:, i:i + 1])
                    nc.scalar.activation(qk_parts[:, 0, f, :], ps[:, bank + f, :], ACT.Identity, bias=bqk[:, f:f + 1],
                                         scale=rescale[:, i:i + 1]).then_inc(qk_ok, 1)

            def v_high(b):
                act.wait_ge(v_ok, b * TT + TT)
                nc.scalar.activation(v_parts[:, 0, :, :], v[:, :, :], ACT.Copy).then_inc(v_hi_ok, 1)

            def exps(b):
                act.wait_ge(bias_ok, b + 1)
                for t in range(TT):
                    nc.scalar.activation(prob[:, t, :], ps[:, 4 + t, :], ACT.Exp, bias=soft_bias[:, t:t + 1],
                                         scale=soft_scale[:, 0:1], accum_out=row_sum[:, t:t + 1]).then_inc(exp_ok, 1)

            def prob_t_high(b):
                for t in range(TT):
                    act.wait_ge(pt_ready, b * TT + (t + 1))
                    nc.scalar.activation(prob_t[:, 0, :, t * P:(t + 1) * P],
                                         ps[:, 4 + t, :].rearrange("p (j s) -> p j s", s=P),
                                         ACT.Copy).then_inc(pt_ok, 1)

            def attn_high(b):
                for d in range(DT):
                    act.wait_ge(pv_ready, b * DT + (d + 1))
                    nc.scalar.activation(attn_t[:, 0, d, bass.ds(b * CH, CH)], ps[:, 6 + d, :], ACT.Copy,
                                         scale=1.0 / PROB_UNIT).then_inc(attn_ok, 1)

            def gu_views(g, par, half, dst):
                if half:
                    return (gu_in[:, 0, g * GU // 2:(g + 1) * GU // 2].rearrange("p (k c) -> p k c", k=KT),
                            dst[:, 0, 0, :, g * HALF:(g + 1) * HALF])
                return gu_in[:, g, :], flat(dst[:, par, g, :, :])

            def gu_high(n, par, half=False):
                act.wait_ge(scales_ok, n + (QKV + 1))
                for g in range(2):
                    w, hi = gu_views(g, par, half, gu_hi)
                    high(w, to_unit[:, par, g:g + 1], hi)

            def gu_low(n, par, half=False):
                for g in range(2):
                    w, lo = gu_views(g, par, half, gu_lo)
                    low(2 * n + (2 * QKV + g + 1), w, to_unit_n[:, par, g:g + 1], lo, lo_sum[:, par, g:g + 1])

            def qkv_high(i):
                act.wait_ge(scales_ok, i + 1)
                for f in range(2 * i, 2 * i + 2):
                    high(wqkv_in[:, f * GU:(f + 1) * GU], to_unit[:, 2 + i, 0:1], flat(wqkv_hi[:, f, :, :]))

            def qkv_low(i):
                for f in range(2 * i, 2 * i + 2):
                    low(f + 1, wqkv_in[:, f * GU:(f + 1) * GU], to_unit_n[:, 2 + i, 0:1], flat(wqkv_lo[:, f, :, :]))

            act.wait_ge(eps_ok, 1)
            nc.scalar.activation(scratch, eps[:, :], ACT.Sqrt)
            std_devs(0)
            act.wait_ge(neg_mean_ok, 1)
            for t in range(2, TT):
                nc.scalar.activation(x_in[:, t, :], x_in[:, t, :], ACT.Identity, bias=neg_mean[:, t - 2:t - 1],
                                     scale=rstd_x[:, t:t + 1]).then_inc(norm_act_ok, 1)
            x_high(0, range(0, 2))
            qkv_high(0)
            x_high(0, range(2, TT))
            for i in range(QKV):
                qkv_low(i)
                if i + 1 < QKV:
                    qkv_high(i + 1)
            std_devs(1)
            act.wait_ge(rescale_ok, 1)
            act.wait_ge(soft_scale_ok, 1)
            act.wait_ge(wlo_ok, 2 * QKV)
            copy_qk(0, bank=4)
            v_high(0)

            def batch(b, more=True):
                x_high(b + 1, range(TT))
                exps(b)
                if more:
                    std_devs(b + 2)
                else:
                    gu_high(0, 0, half=True)
                    gu_low(0, 0, half=True)
                copy_qk(b + 1)
                prob_t_high(b)
                attn_high(b)
                v_high(b + 1)

            with act.Fori(0, B - 2) as b:
                batch(b)
            batch(B - 2, more=False)
            exps(B - 1)

            def magnitude_sign(j, buf, n, src, scale, used, count):
                nonfirst = not (isinstance(j, int) and j < 2)
                if nonfirst:
                    act.wait_ge(rnd_ok, j - 1)
                nc.scalar.activation(mag[0:n, buf, :], src, ACT.Abs, scale=scale).then_inc(mag_ok, 1)
                if nonfirst:
                    act.wait_ge(used, count)
                nc.scalar.activation(sgn[0:n, buf, :], src, ACT.Sign, scale=scale).then_inc(sgn_ok, 1)

            def half_job(c):
                buf, j = c % 2, c
                bank = 2 + c % 2
                act.wait_ge(gu_ready, j + 1)
                nc.scalar.activation(sig[0:HALF, buf, :], ps[0:HALF, bank, :], ACT.Silu,
                                     scale=descale[0:HALF, 0, 0:1])
                if c >= 2:
                    act.wait_ge(rnd_ok, j - 1)
                nc.scalar.activation(mag[0:HALF, buf, :], ps[HALF:P, bank, :], ACT.Copy,
                                     scale=descale[HALF:P, 0, 1:2]).then_inc(silu_ok, 1)
                act.wait_ge(inter_ok, j + 1)
                magnitude_sign(j, buf, HALF, sig[0:HALF, buf, :], 1.0, q_ok, j - 1)

            half_job(0)
            prob_t_high(B - 1)
            gu_high(1, 1)
            half_job(1)
            gu_low(1, 1)
            half_job(2)
            attn_high(B - 1)
            half_job(3)

            def job_b(n, par, c):
                buf, j = c % 2, B * n + c
                act.wait_ge(gu_ready, j + 1)
                nc.scalar.activation(sig[:, buf, :], ps[:, 2 * c, :], ACT.Silu,
                                     scale=descale[:, par, 0:1]).then_inc(silu_ok, 1)
                act.wait_ge(inter_ok, j + 1)
                magnitude_sign(j, buf, P, sig[:, buf, :], 1.0, q_ok, j - 1)

            def tile_b(n, par):
                job_b(n, par, 0)
                gu_high(n + 1, 1 - par)
                gu_low(n + 1, 1 - par)
                for c in range(1, B):
                    job_b(n, par, c)

            with act.Fori(0, NI // 2) as pair:
                tile_b(pair * 2 + 1, 1)
                tile_b(pair * 2 + 2, 0)

            def dn_views(par, piece, dst):
                w, lo, hi = piece
                return w, dst[par][:, lo:hi, :].rearrange("p i c -> p (i c)")

            def dn_high(h, par, places=pieces):
                act.wait_ge(scales_ok, h + (QKV + IT + 1))
                high(wo_in, to_unit[:, par, 1:2], wo_parts[:, par, 0, :])
                for piece in places:
                    w, hi = dn_views(par, piece, dn_hi)
                    high(w, to_unit[:, par, 0:1], hi)

            def wo_low(h, par):
                low(3 * h + (2 * (QKV + IT) + 1), wo_in, to_unit_n[:, par, 1:2], wo_parts[:, par, 1, :])

            def dn_low(h, par, which=(0, 1), places=pieces):
                for g in which:
                    w, lo = dn_views(par, places[g], dn_lo)
                    low(3 * h + (2 * (QKV + IT) + g + 2), w, to_unit_n[:, par, 0:1], lo, lo_sum[:, par, g:g + 1])

            job_b(NI, 1, 0)
            job_b(NI, 1, 1)
            dn_high(0, 0, first_pieces)
            wo_low(0, 0)
            dn_low(0, 0, [0], first_pieces)
            job_b(NI, 1, 2)
            dn_low(0, 0, [1], first_pieces)
            job_b(NI, 1, 3)

            def job_c(h, par, c):
                buf = c % 2
                j = B * h + (JOBS_B + c)
                act.wait_ge(dn_ready, B * h + (c + 1))
                if isinstance(h, int) and B * h + c < 2:
                    used, count = q_ok, JOBS_B + c - 1
                else:
                    used, count = out_ok, B * h + (c - 1)
                magnitude_sign(j, buf, P, ps[:, 2 * c, :], descale[:, par, 0:1], used, count)

            def tile_c(h, par, last=False):
                if not last:
                    dn_high(h + 1, 1 - par)
                job_c(h, par, 0)
                if not last:
                    wo_low(h + 1, 1 - par)
                    dn_low(h + 1, 1 - par)
                for c in range(1, B):
                    job_c(h, par, c)

            tile_c(0, 0)
            with act.Fori(0, (HT - 1 - 1) // 2) as pair:
                h = pair * 2 + 1
                tile_c(h, 1)
                tile_c(h + 1, 0)
            tile_c(HT - 1, 1, last=True)


def kernel(L0_attn_x, L0_attn_Wqkv, L0_attn_bqkv, L0_attn_Wo, L0_attn_bo, L0_ffn_w_gate, L0_ffn_w_up, L0_ffn_w_down):
    import concourse.bacc as bacc
    import numpy as np
    from concourse.bass_utils import run_bass_kernel_spmd

    batch, seq, hid = L0_attn_x.shape
    kt = hid // P
    nf = L0_attn_Wqkv.shape[1] // P
    inner = L0_ffn_w_gate.shape[0]
    ni, half = inner // P, P // 2
    x = np.asarray(L0_attn_x).reshape(batch * seq, hid)
    wqkv = np.asarray(L0_attn_Wqkv).reshape(kt, P, nf, P).transpose(1, 2, 0, 3).reshape(P, nf, kt * P)
    bqkv = np.asarray(L0_attn_bqkv)
    nqk = nf // 3 * 2

    def tiles(w, n):
        return w.reshape(-1, n, kt, P).transpose(0, 3, 2, 1)

    gate, up, down = (np.asarray(w) for w in (L0_ffn_w_gate, L0_ffn_w_up, L0_ffn_w_down))
    w_gu = np.stack([tiles(w[:ni * P], P).reshape(ni, P, kt * P) for w in (gate, up)], axis=2)
    w_gu_last = np.stack([tiles(w[ni * P:], half)[0].reshape(P, kt * half) for w in (gate, up)], axis=1)
    padded = np.zeros((hid, (ni + 1) * P), down.dtype)
    padded[:, :inner] = down
    w_down = padded.reshape(kt, P, ni + 1, P).transpose(0, 3, 2, 1).reshape(kt, P, (ni + 1) * P)
    wo = np.asarray(L0_attn_Wo).reshape(nf // 3, P, kt, P).transpose(2, 1, 0, 3)
    arrays = {
        "x_tok": x,
        "x_feat": x.T.reshape(kt, P, batch * seq),
        "w_qkv": wqkv,
        "b_qk": bqkv[:nqk * P].reshape(nqk, P).T,
        "b_v": bqkv[nqk * P:],
        "w_gu": w_gu,
        "w_gu_last": w_gu_last.reshape(P, kt * P),
        "w_down": w_down,
        "w_o": wo,
        "b_o": np.asarray(L0_attn_bo).reshape(kt, P).T,
    }
    arrays = {k: np.ascontiguousarray(a) for k, a in arrays.items()}
    nc = bacc.Bacc("TRN2", target_bir_lowering=False, num_devices=1)
    args = [nc.dram_tensor(k, a.shape, mybir.dt.from_np(a.dtype), kind="ExternalInput").ap() for k, a in arrays.items()]
    out = nc.dram_tensor("out", (kt, P, batch * seq), F32, kind="ExternalOutput").ap()
    build(nc, *args, out)
    r = run_bass_kernel_spmd(nc, [arrays], core_ids=[0])
    return r.results[0]["out"].reshape(hid, batch, seq).transpose(1, 2, 0)
```
